# Optimizing a Trainium2 kernel written in Bass

```python
import numpy as np
import jax
import jax.numpy as jnp

def _softmax(x, axis=-1):
    return jax.nn.softmax(x, axis=axis)
def _gelu(x):
    return jax.nn.gelu(x, approximate=True)
def _silu(x):
    return jax.nn.silu(x)
def _sigmoid(x):
    return jax.nn.sigmoid(x)
def _layernorm(x, axis=-1, eps=1e-5):
    m = jnp.mean(x, axis=axis, keepdims=True)
    v = jnp.var(x, axis=axis, keepdims=True)
    return (x - m) / jnp.sqrt(v + eps)
def _scatter_add(tgt, idx, src, axis=0):
    return tgt.at[idx].add(src)
def _segment_sum(src, seg, n):
    return jax.ops.segment_sum(src, seg, n)

kernel_name = 'mk_conv_preact_d1_conv_nhwc64_fc53c6'

def setup_inputs(seed: int = 0):
    np.random.seed(seed)
    _w = jnp.asarray
    def _rec_inputs():
        import jax
        import jax.numpy as jnp
        _gk = jax.random.key(seed)
        x = 7.22e-05 + 1 * jax.random.normal(jax.random.fold_in(_gk, 1), (16, 32, 256, 64), jnp.float32)
        return x
    x = _rec_inputs()
    def _L0_conv_setup():
        import jax, jax.numpy as jnp
        import numpy as np
        D_MODEL = 256
        D_FF = 512
        D_STATE = 16
        D_CONV = 4
        EXPAND = 2
        D_INNER = EXPAND * D_MODEL
        DT_RANK = (D_MODEL + 15) // 16
        BSZ = 16
        NVARS = 32
        PATCH_NUM = 64

        def layer_norm(x, g, b, eps=1e-05):
            mu = x.mean(-1, keepdims=True)
            var = ((x - mu) ** 2).mean(-1, keepdims=True)
            return (x - mu) * jax.lax.rsqrt(var + eps) * g + b

        def mamba(x, in_proj_w, in_proj_b, conv_w, conv_b, x_proj_w, dt_proj_w, dt_proj_b, A_log, Dp, out_proj_w):
            b, L, _ = x.shape
            xz = x @ in_proj_w.T + in_proj_b
            xi, z = jnp.split(xz, 2, axis=-1)
            xc = xi.transpose(0, 2, 1)
            xc = jax.lax.conv_general_dilated(xc, conv_w[:, None, :], (1,), [(D_CONV - 1, 0)], dimension_numbers=('NCH', 'OIH', 'NCH'), feature_group_count=D_INNER) + conv_b[None, :, None]
            xi = jax.nn.silu(xc.transpose(0, 2, 1))
            x_dbl = xi @ x_proj_w.T
            dt = x_dbl[..., :DT_RANK]
            B = x_dbl[..., DT_RANK:DT_RANK + D_STATE]
            C = x_dbl[..., DT_RANK + D_STATE:]
            delta = jax.nn.softplus(dt @ dt_proj_w.T + dt_proj_b)
            A = -jnp.exp(A_log)

            def step(h, inp):
                d_t, B_t, C_t, u_t = inp
                dA = jnp.exp(d_t[..., None] * A)
                h = dA * h + (d_t * u_t)[..., None] * B_t[:, None, :]
                y = jnp.einsum('bdn,bn->bd', h, C_t)
                return (h, y)
            h0 = jnp.zeros((b, D_INNER, D_STATE), xi.dtype)
            xs = (delta.transpose(1, 0, 2), B.transpose(1, 0, 2), C.transpose(1, 0, 2), xi.transpose(1, 0, 2))
            _, ys = jax.lax.scan(step, h0, xs)
            y = ys.transpose(1, 0, 2) + xi * Dp
            y = y * jax.nn.silu(z)
            return y @ out_proj_w.T
        key = jax.random.key(seed)
        ks = jax.random.split(key, 16)

        def nrm(k, shape, scale=0.02):
            return jax.random.normal(k, shape, jnp.float32) * scale
        inp = {}
        inp['x'] = jax.random.normal(ks[0], (BSZ, NVARS, D_MODEL, PATCH_NUM), jnp.float32)
        inp['in_proj_w'] = nrm(ks[1], (2 * D_INNER, D_MODEL))
        inp['in_proj_b'] = jnp.zeros((2 * D_INNER,), jnp.float32)
        inp['conv_w'] = nrm(ks[2], (D_INNER, D_CONV), 0.1)
        inp['conv_b'] = jnp.zeros((D_INNER,), jnp.float32)
        inp['x_proj_w'] = nrm(ks[3], (DT_RANK + 2 * D_STATE, D_INNER))
        inp['dt_proj_w'] = nrm(ks[4], (D_INNER, DT_RANK))
        inp['dt_proj_b'] = nrm(ks[5], (D_INNER,), 0.1)
        inp['A_log'] = jnp.log(jnp.broadcast_to(jnp.arange(1, D_STATE + 1, dtype=jnp.float32), (D_INNER, D_STATE)))
        inp['Dp'] = jnp.ones((D_INNER,), jnp.float32)
        inp['out_proj_w'] = nrm(ks[6], (D_MODEL, D_INNER))
        inp['norm1_g'] = jnp.ones((D_MODEL,), jnp.float32)
        inp['norm1_b'] = jnp.zeros((D_MODEL,), jnp.float32)
        inp['ffn1_w'] = nrm(ks[7], (D_FF, D_MODEL))
        inp['ffn1_b'] = jnp.zeros((D_FF,), jnp.float32)
        inp['ffn2_w'] = nrm(ks[8], (D_MODEL, D_FF))
        inp['ffn2_b'] = jnp.zeros((D_MODEL,), jnp.float32)
        inp['norm2_g'] = jnp.ones((D_MODEL,), jnp.float32)
        inp['norm2_b'] = jnp.zeros((D_MODEL,), jnp.float32)
        inp['ln_g'] = jnp.ones((D_MODEL,), jnp.float32)
        inp['ln_b'] = jnp.zeros((D_MODEL,), jnp.float32)
        return inp
    _L0_conv_all = _L0_conv_setup()
    _L0_conv_in = {k: v for k, v in _L0_conv_all.items() if k in ('in_proj_w', 'in_proj_b', 'conv_w', 'conv_b', 'x_proj_w', 'dt_proj_w', 'dt_proj_b', 'A_log', 'Dp', 'out_proj_w', 'norm1_g', 'norm1_b', 'ffn1_w', 'ffn1_b', 'ffn2_w', 'ffn2_b', 'norm2_g', 'norm2_b', 'ln_g', 'ln_b', )}
    del _L0_conv_all

    return {
        "x": x,
        "L0_conv_in_proj_w": _L0_conv_in["in_proj_w"],
        "L0_conv_in_proj_b": _L0_conv_in["in_proj_b"],
        "L0_conv_conv_w": _L0_conv_in["conv_w"],
        "L0_conv_conv_b": _L0_conv_in["conv_b"],
        "L0_conv_x_proj_w": _L0_conv_in["x_proj_w"],
        "L0_conv_dt_proj_w": _L0_conv_in["dt_proj_w"],
        "L0_conv_dt_proj_b": _L0_conv_in["dt_proj_b"],
        "L0_conv_A_log": _L0_conv_in["A_log"],
        "L0_conv_Dp": _L0_conv_in["Dp"],
        "L0_conv_out_proj_w": _L0_conv_in["out_proj_w"],
        "L0_conv_norm1_g": _L0_conv_in["norm1_g"],
        "L0_conv_norm1_b": _L0_conv_in["norm1_b"],
        "L0_conv_ffn1_w": _L0_conv_in["ffn1_w"],
        "L0_conv_ffn1_b": _L0_conv_in["ffn1_b"],
        "L0_conv_ffn2_w": _L0_conv_in["ffn2_w"],
        "L0_conv_ffn2_b": _L0_conv_in["ffn2_b"],
        "L0_conv_norm2_g": _L0_conv_in["norm2_g"],
        "L0_conv_norm2_b": _L0_conv_in["norm2_b"],
        "L0_conv_ln_g": _L0_conv_in["ln_g"],
        "L0_conv_ln_b": _L0_conv_in["ln_b"],
    }

def reference(x, L0_conv_in_proj_w, L0_conv_in_proj_b, L0_conv_conv_w, L0_conv_conv_b, L0_conv_x_proj_w, L0_conv_dt_proj_w, L0_conv_dt_proj_b, L0_conv_A_log, L0_conv_Dp, L0_conv_out_proj_w, L0_conv_norm1_g, L0_conv_norm1_b, L0_conv_ffn1_w, L0_conv_ffn1_b, L0_conv_ffn2_w, L0_conv_ffn2_b, L0_conv_norm2_g, L0_conv_norm2_b, L0_conv_ln_g, L0_conv_ln_b):
    import jax
    import jax.numpy as jnp
    def _L0_conv_ref(x, in_proj_w, in_proj_b, conv_w, conv_b, x_proj_w, dt_proj_w, dt_proj_b, A_log, Dp, out_proj_w, norm1_g, norm1_b, ffn1_w, ffn1_b, ffn2_w, ffn2_b, norm2_g, norm2_b, ln_g, ln_b):
        import jax, jax.numpy as jnp
        import numpy as np
        D_MODEL = 256
        D_FF = 512
        D_STATE = 16
        D_CONV = 4
        EXPAND = 2
        D_INNER = EXPAND * D_MODEL
        DT_RANK = (D_MODEL + 15) // 16
        BSZ = 16
        NVARS = 32
        PATCH_NUM = 64

        def layer_norm(x, g, b, eps=1e-05):
            mu = x.mean(-1, keepdims=True)
            var = ((x - mu) ** 2).mean(-1, keepdims=True)
            return (x - mu) * jax.lax.rsqrt(var + eps) * g + b

        def mamba(x, in_proj_w, in_proj_b, conv_w, conv_b, x_proj_w, dt_proj_w, dt_proj_b, A_log, Dp, out_proj_w):
            b, L, _ = x.shape
            xz = x @ in_proj_w.T + in_proj_b
            xi, z = jnp.split(xz, 2, axis=-1)
            xc = xi.transpose(0, 2, 1)
            xc = jax.lax.conv_general_dilated(xc, conv_w[:, None, :], (1,), [(D_CONV - 1, 0)], dimension_numbers=('NCH', 'OIH', 'NCH'), feature_group_count=D_INNER) + conv_b[None, :, None]
            xi = jax.nn.silu(xc.transpose(0, 2, 1))
            x_dbl = xi @ x_proj_w.T
            dt = x_dbl[..., :DT_RANK]
            B = x_dbl[..., DT_RANK:DT_RANK + D_STATE]
            C = x_dbl[..., DT_RANK + D_STATE:]
            delta = jax.nn.softplus(dt @ dt_proj_w.T + dt_proj_b)
            A = -jnp.exp(A_log)

            def step(h, inp):
                d_t, B_t, C_t, u_t = inp
                dA = jnp.exp(d_t[..., None] * A)
                h = dA * h + (d_t * u_t)[..., None] * B_t[:, None, :]
                y = jnp.einsum('bdn,bn->bd', h, C_t)
                return (h, y)
            h0 = jnp.zeros((b, D_INNER, D_STATE), xi.dtype)
            xs = (delta.transpose(1, 0, 2), B.transpose(1, 0, 2), C.transpose(1, 0, 2), xi.transpose(1, 0, 2))
            _, ys = jax.lax.scan(step, h0, xs)
            y = ys.transpose(1, 0, 2) + xi * Dp
            y = y * jax.nn.silu(z)
            return y @ out_proj_w.T
        b, nv, dm, pn = x.shape
        x_residual = x
        h = x.reshape(b, pn * nv, dm)
        h = h + mamba(h, in_proj_w, in_proj_b, conv_w, conv_b, x_proj_w, dt_proj_w, dt_proj_b, A_log, Dp, out_proj_w)
        h = layer_norm(h, norm1_g, norm1_b)
        y = jax.nn.relu(h @ ffn1_w.T + ffn1_b)
        y = y @ ffn2_w.T + ffn2_b
        h = layer_norm(h + y, norm2_g, norm2_b)
        h = h.reshape(b, nv, pn, dm)
        h = layer_norm(h, ln_g, ln_b).transpose(0, 1, 3, 2)
        return h + x_residual

    def _gn(v, G=32, eps=1e-5):
        B_, H_, W_, C_ = v.shape
        g = v.reshape(B_, H_, W_, G, C_ // G)
        m = jnp.mean(g, axis=(1, 2, 4), keepdims=True)
        s = jnp.var(g, axis=(1, 2, 4), keepdims=True)
        return ((g - m) / jnp.sqrt(s + eps)).reshape(v.shape)

    def _ln_c(v, eps=1e-6):
        m = jnp.mean(v, axis=-1, keepdims=True)
        s = jnp.var(v, axis=-1, keepdims=True)
        return (v - m) / jnp.sqrt(s + eps)

    def _ln_t(v, eps=1e-5):
        m = jnp.mean(v, axis=-1, keepdims=True)
        s = jnp.var(v, axis=-1, keepdims=True)
        return (v - m) / jnp.sqrt(s + eps)

    def _to_tokens(v):
        B_, H_, W_, C_ = v.shape
        return v.reshape(B_, H_ * W_, C_)
    def _from_tokens(t, like):
        return t.reshape(like.shape)

    x = x + _L0_conv_ref(_gn(x), L0_conv_in_proj_w, L0_conv_in_proj_b, L0_conv_conv_w, L0_conv_conv_b, L0_conv_x_proj_w, L0_conv_dt_proj_w, L0_conv_dt_proj_b, L0_conv_A_log, L0_conv_Dp, L0_conv_out_proj_w, L0_conv_norm1_g, L0_conv_norm1_b, L0_conv_ffn1_w, L0_conv_ffn1_b, L0_conv_ffn2_w, L0_conv_ffn2_b, L0_conv_norm2_g, L0_conv_norm2_b, L0_conv_ln_g, L0_conv_ln_b)
    return x


_drawn_inputs = setup_inputs


def setup_inputs(seed=0):
    import zlib

    import numpy as np

    out = dict(_drawn_inputs(seed))
    spreads = {'L0_conv_in_proj_b': (0.0, 0.8),
     'L0_conv_conv_b': (0.0, 0.8),
     'L0_conv_Dp': (1.0, 0.6),
     'L0_conv_norm1_g': (1.0, 0.2),
     'L0_conv_norm1_b': (0.0, 0.1),
     'L0_conv_ffn1_b': (0.0, 0.646),
     'L0_conv_ffn2_b': (0.0, 0.1),
     'L0_conv_norm2_g': (1.0, 0.2),
     'L0_conv_norm2_b': (0.0, 0.1),
     'L0_conv_ln_g': (1.0, 0.2),
     'L0_conv_ln_b': (0.0, 0.1)}
    factors = {'L0_conv_in_proj_w': 8.0,
     'L0_conv_conv_w': 8.0,
     'L0_conv_x_proj_w': 8.0,
     'L0_conv_dt_proj_w': 8.0,
     'L0_conv_dt_proj_b': 8.0,
     'L0_conv_A_log': 8.0,
     'L0_conv_out_proj_w': 8.0}
    for name, (base, spread) in spreads.items():
        noise = np.random.default_rng([zlib.crc32(name.encode()), seed]).standard_normal(out[name].shape)
        drawn = base * np.exp(spread * noise) if base else spread * noise
        out[name] = jnp.asarray(drawn.astype(out[name].dtype))
    for name, factor in factors.items():
        out[name] = (out[name] * factor).astype(out[name].dtype)
    return out
```

```python
from contextlib import ExitStack

import concourse.bass as bass
from concourse import mybir

F32 = mybir.dt.float32
BF16 = mybir.dt.bfloat16
ALU = mybir.AluOpType
ACT = mybir.ActivationFunctionType

P = 128
DM, DI, DF, NS, R, KC = 256, 512, 512, 16, 16, 4
T = 512
Q = T // P
JB = DI // P
FB = DM // P
MB = DF // P
SEQ, BATCH, CH = 2048, 16, 64
CHUNKS = BATCH * SEQ // T
PAIRS = CHUNKS // 2
STEPS = NS * JB
FIRST_LOOPED = 2
NBB = 4
EPS = 1e-5
LN_SET = "natural_log_exp_and_others"
SILU_SET = "silu_and_others"

DA0, HT0, FR0, BK0 = 0, 2, 4, 6

G_XT, G_XI, G_Z, G_XD, G_C, G_DT = 0, 2, 6, 10, 11, 12
GF = 16
K_YT, K_OUT, K_N1T, K_FF1, K_FF2 = 0, 4, 6, 8, 12
GB = 14
E_R, E_N3T = 0, 1
GE = 3
LN_NORM, LN_ALL = 13, 39
STEPS_SP = 4
GN_DEV, GN_VAR, GN_V, GN_DONE = 1, 6, 7, 12


def layer_kernel(nc, x, consts, win_t, bin_c, convw, convb, wx, wc, wdt, alog, dpar, wout, n1g, n1b,
                 wf1, bf1, wf2, bf2, g2rows, b2rows, lng, lnb, out):
    x_tok = x.rearrange("b v (w r) c -> (b v w) (r c)", r=DM // CH).rearrange(
        "(c q p) f -> c p q f", p=P, q=Q)
    x_nat = x.rearrange("b (k v) (f w) c -> (b k) f w v c", k=SEQ // T, f=FB)
    o_nat = out.rearrange("b (k v) (f w) c -> (b k) f w v c", k=SEQ // T, f=FB)
    x_seq = x.rearrange("b v (w r) c -> b (v w) (r c)", r=DM // CH).rearrange(
        "b (q p) f -> b p q f", p=P)

    with ExitStack() as ctx:
        def sb(name, shape, dt=F32):
            return ctx.enter_context(nc.sbuf_tensor(name, shape, dt))

        def sem(name):
            return ctx.enter_context(nc.semaphore(name))

        ps = ctx.enter_context(nc.psum_tensor("ps", [P, 8, 512], F32))

        cst = sb("cst", [P, 2 * P + PAIRS + 1])
        ident = cst[:, 0:P]
        group_avg = cst[:, P:2 * P]
        starts = cst[:, 2 * P:]
        mask = sb("mask", [P, 2])
        ones = sb("ones", [P, P])
        w_in = sb("w_in", [P, FB, 2 * DI])
        b_in = sb("b_in", [P, 2 * JB])
        w_cv = sb("w_cv", [P, JB, KC])
        b_cv = sb("b_cv", [P, JB])
        w_x = sb("w_x", [P, JB, P])
        w_c = sb("w_c", [P, JB, NS])
        w_dt = sb("w_dt", [P, DI])
        a_neg = sb("a_neg", [P, JB, NS])
        d_par = sb("d_par", [P, JB])
        w_out = sb("w_out", [P, JB, DM])
        n1_g = sb("n1_g", [P, FB])
        n1_b = sb("n1_b", [P, FB])
        w_f1 = sb("w_f1", [P, FB, DF])
        b_f1 = sb("b_f1", [P, MB])
        w_f2 = sb("w_f2", [P, MB, DM])
        b_f2 = sb("b_f2", [P, DM])
        n2_g = sb("n2_g", [P, DM])
        n2_b = sb("n2_b", [P, DM])
        ln_g = sb("ln_g", [P, FB])
        ln_b = sb("ln_b", [P, FB])

        xt = sb("xt", [P, Q, DM])
        coef = sb("coef", [P, PAIRS, 4])
        coef_c = sb("coef_c", [P, 2, 4])
        coef_e = sb("coef_e", [P, 4])
        xn = sb("xn", [P, 2, FB, T])
        xi = sb("xi", [P, JB, KC - 1 + T])
        u = sb("u", [P, 2, JB, T])
        sz = sb("sz", [P, 2, JB, T])
        v = sb("v", [P, JB, T])
        xd = sb("xd", [P, 2, T])
        cs = sb("cs", [P, 2, Q, NS])
        sp_e = v
        sp_l = sb("sp_l", [P, 2, T])
        sp_m = sb("sp_m", [P, T])
        delta = sb("delta", [P, 2, JB, T])
        du = sb("du", [P, JB, T])
        bb = sb("bb", [P, NBB, T])
        dbu = sb("dbu", [P, 2, JB, T])
        h = sb("h", [P, 2, JB, T])
        carry = sb("carry", [P, NS, JB])
        y = sb("y", [P, 2, Q, DI])
        xres = sb("xres", [P, FB, T])
        st = sb("st", [P, 3, Q, 6])
        mv = sb("mv", [P, 3, Q, 2])
        rs = sb("rs", [P, 3, Q])
        rt = sb("rt", [P, 3, Q])
        eps = sb("eps", [P, 1])
        nrm = sb("nrm", [P, Q, DM])
        h1 = sb("h1", [P, FB, T])
        ff = sb("ff", [P, MB, T])
        rdiag = sb("rdiag", [P, 2 * CH])
        rrow = sb("rrow", [P, 2 * CH])
        xw = sb("xw", [P, FB, T])
        o = xt[:, :, :].rearrange("p (f a) d -> p f (a d)", f=FB)
        stats = du[:, :, :].rearrange("p j t -> p (j t)")[:, 0:FB * BATCH * 24].rearrange(
            "p (f b s) -> p f b s", f=FB, b=BATCH)
        seq_buf = [u[:, :, :, :].rearrange("p a j t -> p (a j t)").rearrange("p (q f) -> p q f", f=DM),
                   sz[:, :, :, :].rearrange("p a j t -> p (a j t)").rearrange("p (q f) -> p q f", f=DM)]
        mvs = sb("mvs", [P, FB, BATCH, 2])
        gn = sb("gn", [P, 6, BATCH])

        w_loaded = sem("w_loaded")
        seq_in = [sem("seq_in0"), sem("seq_in1")]
        seq_turned, seq_stat = sem("seq_turned"), sem("seq_stat")
        gn_aggr, gn_step, gn_mm, gn_root = sem("gn_aggr"), sem("gn_step"), sem("gn_mm"), sem("gn_root")
        prep_act, prep_dve = sem("prep_act"), sem("prep_dve")
        x_in, xw_in, stored = sem("x_in"), sem("xw_in"), sem("stored")
        front_mm, back_mm, end_mm = sem("front_mm"), sem("back_mm"), sem("end_mm")
        coef_set, ctx_set, mask_set = sem("coef_set"), sem("ctx_set"), sem("mask_set")
        xn_set, xi_set, tap_set, conv_step, z_set, silu_set = (
            sem(n) for n in ("xn_set", "xi_set", "tap_set", "conv_step", "z_set", "silu_set"))
        xd_set, cs_set, xres_set, nrm_set = sem("xd_set"), sem("cs_set"), sem("xres_set"), sem("nrm_set")
        sp_abs, sp_relu, sp_exp, sp_log, sp_step = (sem(n) for n in ("sp_abs", "sp_relu", "sp_exp", "sp_log", "sp_step"))
        bb_in = [sem(f"bb_in{k}") for k in range(NBB)]
        du_set, dbu_set = sem("du_set"), sem("dbu_set")
        da_set, scanned, carried, turned, summed = (sem(n) for n in ("da_set", "scanned", "carried", "turned", "summed"))
        rdiag_set, rrow_set, skip_set, gated = sem("rdiag_set"), sem("rrow_set"), sem("skip_set"), sem("gated")
        ln_step, root_step, h1_set, ff_set, affine_step, o_set, resid_step = (
            sem(n) for n in ("ln_step", "root_step", "h1_set", "ff_set", "affine_step", "o_set", "resid_step"))

        block = ctx.enter_context(nc.Block())

        def wait(eng, s, c, per, n):
            i, k = c
            if isinstance(i, int):
                v = (2 * i + k) * per + n
                if v > 0:
                    eng.wait_ge(s, v)
            else:
                assert 2 * FIRST_LOOPED * per + k * per + n > 0
                eng.wait_ge(s, i * (2 * per) + (k * per + n))

        def wait_both(eng, a, b):
            values = []
            for s, (i, k), per, n in (a, b):
                assert 2 * FIRST_LOOPED * per + k * per + n > 0 or isinstance(i, int)
                v = i * (2 * per) + (k * per + n)
                values.append((s, v if isinstance(i, int) else eng.to_reg(v)))
            for s, v in values:
                if not isinstance(v, int) or v > 0:
                    eng.wait_ge(s, v)

        def after(c, d):
            return (c[0], c[1] + d)

        def par(c):
            return c[1] % 2

        def pair_of(c):
            i, k = c
            return i + k // 2

        def is_first(c):
            return isinstance(c[0], int) and 2 * c[0] + c[1] == 0

        def periods(eng, period):
            every = ("scan", "front", "back", "end")
            period((0, 0), ("scan", "front"))
            period((0, 1), ("scan", "front", "back"))
            period((1, 0), every)
            period((1, 1), every)
            with eng.Fori(FIRST_LOOPED, PAIRS - 1) as i:
                period((i, 0), every)
                period((i, 1), every)
            period((PAIRS - 1, 0), every)
            period((PAIRS - 1, 1), ("scan", "back", "end"))
            period((PAIRS - 1, 2), ("back", "end"))
            period((PAIRS - 1, 3), ("end",))

        @block.sync
        def _(sp):
            for dst, src in (
                    (cst[:, :], consts), (w_in[:, :, :], win_t.rearrange("(f p) e -> p f e", p=P)),
                    (b_in[:, :], bin_c),
                    (w_cv[:, :, :], convw.rearrange("(j p) k -> p j k", p=P)),
                    (b_cv[:, :], convb),
                    (w_x[:, :, :], wx.rearrange("(j p) m -> p j m", p=P)),
                    (w_c[:, :, :], wc.rearrange("(j p) m -> p j m", p=P)),
                    (w_dt[96:96 + R + 1, :], wdt),
                    (a_neg[:, :, :], alog.rearrange("(j p) n -> p j n", p=P)),
                    (d_par[:, :], dpar),
                    (w_out[:, :, :], wout.rearrange("(j p) m -> p j m", p=P)),
                    (n1_g[:, :], n1g),
                    (n1_b[:, :], n1b),
                    (w_f1[:, :, :], wf1.rearrange("(f p) m -> p f m", p=P)),
                    (b_f1[:, :], bf1),
                    (w_f2[:, :, :], wf2.rearrange("(j p) m -> p j m", p=P)),
                    (b_f2[0:1, :], bf2.rearrange("(a m) -> a m", a=1)),
                    (n2_g[:, :], g2rows), (n2_b[:, :], b2rows),
                    (ln_g[:, :], lng),
                    (ln_b[:, :], lnb)):
                sp.dma_start(dst, src).then_inc(w_loaded, 16)

            def load_sequences(i):
                for k in range(2):
                    wait(sp, seq_turned, (i, k), 8, -8)
                    sp.dma_start(seq_buf[k], x_seq[2 * i + k]).then_inc(seq_in[k], 16)
            load_sequences(0)
            with sp.Fori(1, BATCH // 2) as i:
                load_sequences(i)

            def load_x(c):
                wait_both(sp, (front_mm, after(c, -1), GF, G_XI),
                          (stored, after(c, -3), 32, 0))
                i, k = c
                sp.dma_start(xt[:, :, :], x_tok[2 * i + k]).then_inc(x_in, 16)

            def load_residual(c):
                i, k = c
                wait(sp, resid_step, c, 3, 0)
                for f in range(FB):
                    sp.dma_start(xw[:, f, :].rearrange("p (v c) -> p v c", c=CH),
                                 x_nat[2 * i + k, f]).then_inc(xw_in, 16)

            def store(c):
                i, k = c
                wait(sp, resid_step, c, 3, 3)
                for f in range(FB):
                    sp.dma_start(o_nat[2 * i + k, f],
                                 o[:, f, :].rearrange("p (v c) -> p v c", c=CH)).then_inc(stored, 16)

            def spread_b(c, n):
                used = (dbu_set, c, NS, n - NBB + 1)
                if n == 0:
                    wait_both(sp, (xd_set, c, 1, 1), used)
                else:
                    wait(sp, *used)
                sp.dma_start(bb[:, n % NBB, :], xd[n:n + 1, par(c), :].unsqueeze(1).broadcast_to([1, P, T])).then_inc(bb_in[n % NBB], 16)

            load_x((0, 0))
            for n in range(NBB - 1):
                spread_b((0, 0), n)

            def period(c, parts):
                for n in range(NS):
                    if "scan" in parts and n + NBB - 1 < NS:
                        spread_b(c, n + NBB - 1)
                    if "front" in parts and n == 0:
                        load_x(after(c, 1))
                    if "front" in parts and n + NBB - 1 >= NS:
                        spread_b(after(c, 1), n + NBB - 1 - NS)
                    if "end" in parts and n == 1: load_residual(after(c, -2))
                    if "end" in parts and n == 9: store(after(c, -2))
            periods(sp, period)
            sp.wait_ge(stored, 32 * CHUNKS)

        FRONT_ORDER = ([("end", E_R)] + [("front", k) for k in range(G_Z + 2)] + [("end", E_N3T), ("end", E_N3T + 1)]
                       + [("front", k) for k in range(G_Z + 2, GF)])

        def front_bank(g):
            return FR0 + FRONT_ORDER.index(g) % 2

        @block.tensor
        def _(pe):
            pe.wait_ge(w_loaded, 16 * 21)

            def turn_sequences(i):
                for k in range(2):
                    wait(pe, seq_in[k], (i, 0), 8, 16)
                    for g in range(8):
                        f, r = g // 4, g % 4
                        wait(pe, seq_stat, (i, k), 8, g - 7)
                        for t in range(4):
                            mm = pe.transpose(ps[:, g, t * P:(t + 1) * P],
                                              seq_buf[k][:, 4 * r + t, f * P:(f + 1) * P], ident)
                        mm.then_inc(seq_turned, 1)
            turn_sequences(0)
            with pe.Fori(1, BATCH // 2) as i:
                turn_sequences(i)

            def average(src, bank, value):
                pe.wait_ge(gn_step, value)
                for f in range(FB):
                    mm = pe.matmul(ps[:, bank, 0:BATCH], group_avg, src(f), start=(f == 0), stop=(f == FB - 1))
                mm.then_inc(gn_mm, 1)
            pe.wait_ge(gn_aggr, FB * BATCH)
            pe.wait_ge(seq_stat, 8 * BATCH)
            average(lambda f: mvs[:, f, :, 0], 0, GN_DEV)
            average(lambda f: mvs[:, f, :, 1], 1, GN_VAR)
            pe.wait_ge(prep_dve, 5)

            def front_read(k, c):
                if k < G_XI:
                    wait(pe, xn_set, c, FB, k + 1)
                elif k < G_Z:
                    wait(pe, xi_set, c, JB, k - G_XI + 1)
                elif k < G_XD:
                    wait(pe, z_set, c, JB, k - G_Z + 1)
                elif k == G_XD:
                    wait(pe, xd_set, c, 1, 1)
                elif k == G_C:
                    wait(pe, cs_set, c, 1, 1)
                else:
                    wait(pe, sp_abs, c, JB, k - G_DT + 1)
                    wait(pe, sp_relu, c, JB, k - G_DT + 1)

            def end_read(k, c):
                if k == E_R:
                    wait(pe, rrow_set, c, 1, 1)
                else:
                    wait(pe, o_set, c, FB, k - E_N3T + 1)

            def exists(c):
                return not isinstance(c[0], int) or 0 <= 2 * c[0] + c[1] < CHUNKS

            def front_free(g, c):
                at = FRONT_ORDER.index(g)
                users = [(x, 0) for x in FRONT_ORDER[:at]][::-1] + [(x, -1) for x in FRONT_ORDER[::-1]]
                for x, d in users:
                    kind, k = x
                    chunk = after(c, d + (1 if kind == "front" else -2))
                    if front_bank(x) == front_bank(g) and exists(chunk):
                        (front_read if kind == "front" else end_read)(k, chunk)
                        return

            def bank(kind, k):
                return ps[:, front_bank((kind, k)), :]

            def turn_x(c, f):
                if f == 0:
                    wait(pe, x_in, c, 16, 16)
                front_free(("front", G_XT + f), after(c, -1))
                for q in range(Q):
                    mm = pe.transpose(bank("front", G_XT + f)[:, q * P:(q + 1) * P], xt[:, q, f * P:(f + 1) * P], ident)
                mm.then_inc(front_mm, 1)

            def in_proj(c, j):
                g = G_XI + j
                if j == 0:
                    wait(pe, xn_set, c, FB, FB)
                front_free(("front", g), after(c, -1))
                for f in range(FB):
                    mm = pe.matmul(bank("front", g), w_in[:, f, j * P:(j + 1) * P], xn[:, par(c), f, :],
                                   start=(f == 0), stop=(f == FB - 1))
                mm.then_inc(front_mm, 1)

            def x_proj(c):
                wait(pe, silu_set, c, 2, 1)
                front_free(("front", G_XD), after(c, -1))
                for j in range(JB):
                    mm = pe.matmul(bank("front", G_XD), w_x[:, j, :], u[:, par(c), j, :],
                                   start=(j == 0), stop=(j == JB - 1))
                mm.then_inc(front_mm, 1)

            def c_proj(c):
                front_free(("front", G_C), after(c, -1))
                for q in range(Q):
                    for j in range(JB):
                        mm = pe.matmul(bank("front", G_C)[:, q * NS:(q + 1) * NS], u[:, par(c), j, q * P:(q + 1) * P],
                                       w_c[:, j, :], start=(j == 0), stop=(j == JB - 1))
                mm.then_inc(front_mm, 1)

            def dt_proj(c, j):
                if j == 0:
                    wait(pe, xd_set, c, 1, 1)
                front_free(("front", G_DT + j), after(c, -1))
                pe.matmul(bank("front", G_DT + j), w_dt[96:96 + R + 1, j * P:(j + 1) * P],
                          xd[96:96 + R + 1, par(c), :], start=True, stop=True).then_inc(front_mm, 1)

            def turn_h(c, n, q):
                if q == 0:
                    wait(pe, scanned, c, STEPS, 4 * n + 4)
                wait(pe, summed, c, STEPS, 4 * n + q - 1)
                for j in range(JB):
                    mm = pe.transpose(ps[:, HT0 + q % 2, j * P:(j + 1) * P], h[:, n % 2, j, q * P:(q + 1) * P], ident)
                mm.then_inc(turned, 1)

            def back_bank(k):
                return ps[:, BK0 + k % 2, :]

            def back_free(k, c):
                k, c = (k - 2, c) if k >= 2 else (k - 2 + GB, after(c, -1))
                if k < K_OUT:
                    wait(pe, skip_set, c, JB, k - K_YT + 1)
                elif k < K_N1T:
                    wait(pe, nrm_set, c, 3 * Q, 2 * (k - K_OUT + 1))
                elif k < K_FF1:
                    wait(pe, h1_set, c, FB, k - K_N1T + 1)
                elif k < K_FF2:
                    wait(pe, ff_set, c, MB, k - K_FF1 + 1)
                else:
                    wait(pe, nrm_set, c, 3 * Q, Q + 2 * (k - K_FF2 + 1))

            def turn_y(c, j):
                wait(pe, summed, c, STEPS, STEPS)
                back_free(K_YT + j, c)
                for q in range(Q):
                    mm = pe.transpose(back_bank(K_YT + j)[:, q * P:(q + 1) * P], y[:, par(c), q, j * P:(j + 1) * P],
                                      ident)
                mm.then_inc(back_mm, 1)

            def out_proj(c, q):
                g, r = q // 2, q % 2
                if r == 0:
                    wait(pe, gated, c, JB, JB)
                    wait(pe, xres_set, c, FB, FB)
                    back_free(K_OUT + g, c)
                dst = back_bank(K_OUT + g)
                for j in range(JB):
                    pe.matmul(dst[:, r * DM:(r + 1) * DM], u[:, par(c), j, q * P:(q + 1) * P], w_out[:, j, :],
                              start=(j == 0), stop=False)
                for f in range(FB):
                    mm = pe.matmul(dst[:, r * DM + f * P:r * DM + (f + 1) * P], xres[:, f, q * P:(q + 1) * P], ident,
                                   start=False, stop=(f == FB - 1))
                if r == 1:
                    mm.then_inc(back_mm, 1)

            def turn_norm(c, f):
                wait(pe, nrm_set, c, 3 * Q, Q)
                back_free(K_N1T + f, c)
                for q in range(Q):
                    mm = pe.transpose(back_bank(K_N1T + f)[:, q * P:(q + 1) * P], nrm[:, q, f * P:(f + 1) * P], ident)
                mm.then_inc(back_mm, 1)

            def ffn1(c, m):
                wait(pe, h1_set, c, FB, FB)
                back_free(K_FF1 + m, c)
                for f in range(FB):
                    mm = pe.matmul(back_bank(K_FF1 + m), w_f1[:, f, m * P:(m + 1) * P], h1[:, f, :],
                                   start=(f == 0), stop=(f == FB - 1))
                mm.then_inc(back_mm, 1)

            def ffn2(c, q):
                g, r = q // 2, q % 2
                if r == 0:
                    wait(pe, ff_set, c, MB, MB)
                    back_free(K_FF2 + g, c)
                dst = back_bank(K_FF2 + g)
                for m in range(MB):
                    pe.matmul(dst[:, r * DM:(r + 1) * DM], ff[:, m, q * P:(q + 1) * P], w_f2[:, m, :],
                              start=(m == 0), stop=False)
                pe.matmul(dst[:, r * DM:(r + 1) * DM], ones[0:1, :], b_f2[0:1, :], start=False, stop=False)
                for f in range(FB):
                    mm = pe.matmul(dst[:, r * DM + f * P:r * DM + (f + 1) * P], h1[:, f, q * P:(q + 1) * P], ident,
                                   start=False, stop=(f == FB - 1))
                if r == 1:
                    mm.then_inc(back_mm, 1)

            def spread_r(c):
                wait(pe, rdiag_set, c, 3, 3)
                front_free(("end", E_R), after(c, 2))
                pe.matmul(bank("end", E_R)[:, 0:2 * CH], ones[0:CH, :], rdiag[0:CH, :],
                          start=True, stop=True).then_inc(end_mm, 1)

            def turn_last(c, f):
                wait(pe, nrm_set, c, 3 * Q, 3 * Q)
                front_free(("end", E_N3T + f), after(c, 2))
                for q in range(Q):
                    mm = pe.transpose(bank("end", E_N3T + f)[:, q * P:(q + 1) * P], nrm[:, q, f * P:(f + 1) * P], ident)
                mm.then_inc(end_mm, 1)

            def end_step(c, s):
                if s == 1: spread_r(c)
                if s in (29, 30): turn_last(c, s - 29)

            def back_step(c, s):
                if s in (8, 9): turn_y(c, s - 8)
                if s in (14, 15): turn_y(c, 2 + s - 14)
                if s in (26, 27): out_proj(c, s - 26)
                if s in (32, 33): out_proj(c, s - 30)
                if s in (43, 44): turn_norm(c, s - 43)
                if s in (48, 49, 50, 51): ffn1(c, s - 48)
                if s in (56, 57, 58, 59): ffn2(c, s - 56)

            def front_step(c, s):
                if s in (10, 11): turn_x(c, s - 10)
                if s in (16, 18, 20, 22): in_proj(c, (s - 16) // 2)
                if s in (24, 25): in_proj(c, JB + s - 24)
                if s in (34, 35): in_proj(c, JB + s - 32)
                if s == 39: x_proj(c)
                if s == 41: c_proj(c)
                if s in (45, 46, 52, 53): dt_proj(c, (45, 46, 52, 53).index(s))

            for s in range(STEPS):
                front_step((0, 0), s)

            def period(c, parts):
                for s in range(STEPS):
                    if s >= 4 and "scan" in parts:
                        turn_h(c, s // 4 - 1, s % 4)
                    if s < 4 and "back" in parts:
                        turn_h(after(c, -1), NS - 1, s)
                    if "end" in parts: end_step(after(c, -2), s)
                    if "back" in parts: back_step(after(c, -1), s)
                    if "front" in parts: front_step(after(c, 1), s)
            periods(pe, period)

        @block.scalar
        def _(act):
            nc.scalar.preload_act_table_set(LN_SET)
            act.wait_ge(w_loaded, 16 * 21)
            act.activation(a_neg[:, :, :], a_neg[:, :, :], ACT.Exp).then_inc(prep_act, 1)
            act.wait_ge(prep_dve, 5)
            act.wait_ge(gn_step, GN_V)
            act.activation(gn[:, 3, :], gn[:, 2, :], ACT.Ln).then_inc(gn_root, 1)
            act.wait_ge(gn_root, 1)
            act.activation(gn[:, 1, :], gn[:, 3, :], ACT.Exp, scale=-0.5).then_inc(gn_root, 1)
            act.wait_ge(gn_step, GN_DONE)

            def bank(kind, k):
                return ps[:, front_bank((kind, k)), :]

            def back_bank(k):
                return ps[:, BK0 + k % 2, :]

            def scale_x(c, f):
                wait(act, front_mm, c, GF, G_XT + f + 1)
                wait(act, coef_set, c, 1, 1)
                wait(act, xres_set, after(c, -2), FB, FB)
                k = coef_c[:, par(c), :]
                act.activation(xn[:, par(c), f, :], bank("front", G_XT + f), ACT.Identity,
                               scale=k[:, 0:1], bias=k[:, 1:2]).then_inc(xn_set, 1)

            def keep_xres(c, f):
                wait(act, back_mm, after(c, -1), GB, K_N1T)
                wait(act, xn_set, c, FB, FB)
                act.activation(xres[:, f, :], xn[:, par(c), f, :], ACT.Identity).then_inc(xres_set, 1)

            def keep_xi(c, j):
                wait(act, front_mm, c, GF, G_XI + j + 1)
                wait(act, ctx_set, c, 1, 1)
                act.activation(xi[:, j, KC - 1:], bank("front", G_XI + j), ACT.Identity,
                               bias=b_in[:, j:j + 1]).then_inc(xi_set, 1)

            def last_tap(c, j):
                wait(act, xi_set, c, JB, j + 1)
                wait(act, sp_step, c, JB * STEPS_SP, 0)
                act.activation(v[:, j, :], xi[:, j, KC - 1:], ACT.Identity, scale=w_cv[:, j, KC - 1:KC],
                               bias=b_cv[:, j:j + 1]).then_inc(tap_set, 1)

            def keep_z(c, j):
                wait(act, front_mm, c, GF, G_Z + j + 1)
                wait(act, gated, after(c, -2), JB, JB)
                act.activation(sz[:, par(c), j, :], bank("front", G_Z + j), ACT.Identity,
                               bias=b_in[:, JB + j:JB + j + 1]).then_inc(z_set, 1)

            def silu(c):
                nc.scalar.preload_act_table_set(SILU_SET)
                wait(act, conv_step, c, JB * (KC - 1), JB * (KC - 1))
                wait(act, back_mm, after(c, -2), GB, K_N1T)
                act.activation(u[:, par(c), :, :], v[:, :, :], ACT.Silu).then_inc(silu_set, 1)
                wait(act, z_set, c, JB, JB)
                act.activation(sz[:, par(c), :, :], sz[:, par(c), :, :], ACT.Silu).then_inc(silu_set, 1)
                nc.scalar.preload_act_table_set(LN_SET)

            def keep_xd(c):
                wait(act, front_mm, c, GF, G_XD + 1)
                wait(act, dbu_set, after(c, -1), NS, 0)
                act.activation(xd[0:96 + R, par(c), :], bank("front", G_XD)[0:96 + R, :], ACT.Identity
                               ).then_inc(xd_set, 1)

            def keep_c(c):
                wait(act, front_mm, c, GF, G_C + 1)
                wait(act, summed, after(c, -2), STEPS, STEPS)
                act.activation(cs[:, par(c), :, :], bank("front", G_C)[:, 0:Q * NS], ACT.Identity).then_inc(cs_set, 1)

            def soft_split(c, j):
                wait(act, front_mm, c, GF, G_DT + j + 1)
                wait(act, silu_set, c, 2, 1)
                act.activation(sp_e[:, j, :], bank("front", G_DT + j), ACT.Abs).then_inc(sp_abs, 1)
                wait(act, da_set, after(c, -1), STEPS, 0)
                wait(act, du_set, after(c, -1), JB, 0)
                act.activation(delta[:, par(c), j, :], bank("front", G_DT + j), ACT.Relu).then_inc(sp_relu, 1)

            def soft_exp(c, j):
                wait(act, sp_abs, c, JB, j + 1)
                act.activation(sp_e[:, j, :], sp_e[:, j, :], ACT.Exp, scale=-1.0).then_inc(sp_exp, 1)

            def soft_log(c, j):
                wait(act, sp_exp, c, JB, j + 1)
                wait(act, sp_step, c, JB * STEPS_SP, STEPS_SP * (j - 1) - 2)
                act.activation(sp_l[:, j % 2, :], sp_e[:, j, :], ACT.Ln, bias=1.0).then_inc(sp_log, 1)

            def decay(c, s):
                n, j = s // JB, s % JB
                if s == 0:
                    wait(act, sp_step, c, JB * STEPS_SP, JB * STEPS_SP)
                wait(act, scanned, c, STEPS, s - 1)
                act.activation(ps[:, DA0 + s % 2, :], delta[:, par(c), j, :], ACT.Exp,
                               scale=a_neg[:, j, n:n + 1]).then_inc(da_set, 1)

            def root(c, k):
                wait(act, ln_step, c, LN_ALL, LN_NORM * k + 2 * Q)
                wait(act, nrm_set, c, 3 * Q, Q * k)
                act.activation(rs[:, k, :], mv[:, k, :, 1], ACT.Ln, bias=eps[:, 0:1]).then_inc(root_step, 1)
                wait(act, root_step, c, 6, 2 * k + 1)
                act.activation(rs[:, k, :], rs[:, k, :], ACT.Exp, scale=-0.5).then_inc(root_step, 1)

            def norm(c, k, g):
                wait(act, ln_step, c, LN_ALL, LN_NORM * (k + 1))
                if k == 0:
                    wait(act, end_mm, after(c, -1), GE, GE)
                if k == 1:
                    wait(act, back_mm, c, GB, K_FF1)
                for r in range(2):
                    q = 2 * g + r
                    src = nrm[:, q, :] if k == 2 else back_bank((K_OUT, K_FF2)[k] + g)[:, r * DM:(r + 1) * DM]
                    act.activation(nrm[:, q, :], src, ACT.Identity, scale=rs[:, k, q:q + 1],
                                   bias=rt[:, k, q:q + 1]).then_inc(nrm_set, 1)

            def keep_h1(c, f):
                wait(act, back_mm, c, GB, K_N1T + f + 1)
                wait(act, back_mm, after(c, -1), GB, GB)
                act.activation(h1[:, f, :], back_bank(K_N1T + f), ACT.Identity, scale=n1_g[:, f:f + 1],
                               bias=n1_b[:, f:f + 1]).then_inc(h1_set, 1)

            def keep_ff(c, m):
                wait(act, back_mm, c, GB, K_FF1 + m + 1)
                act.activation(ff[:, m, :], back_bank(K_FF1 + m), ACT.Relu, bias=b_f1[:, m:m + 1]).then_inc(ff_set, 1)

            def keep_r(c):
                wait(act, end_mm, c, GE, E_R + 1)
                wait(act, resid_step, c, 3, 0)
                act.activation(rrow[:, :], bank("end", E_R)[:, 0:2 * CH], ACT.Identity).then_inc(rrow_set, 1)

            def keep_o(c, f, last):
                wait(act, end_mm, c, GE, E_N3T + f + 1)
                if last:
                    act.wait_ge(front_mm, GF * CHUNKS)
                else:
                    wait(act, front_mm, after(c, 3), GF, G_XI)
                act.activation(o[:, f, :], bank("end", E_N3T + f), ACT.Identity, scale=ln_g[:, f:f + 1],
                               bias=ln_b[:, f:f + 1]).then_inc(o_set, 1)

            def end_step(c, s, last):
                if s == 2:
                    root(c, 1)
                    keep_r(c)
                if s in (5, 6): norm(c, 1, s - 5)
                if s == 21: root(c, 2)
                if s in (25, 26): norm(c, 2, s - 25)
                if s in (31, 32): keep_o(c, s - 31, last)

            def back_step(c, s):
                if s in (0, 1): keep_xres(c, s)
                if s == 37: root(c, 0)
                if s in (40, 41): norm(c, 0, s - 40)
                if s in (45, 46): keep_h1(c, s - 45)
                if s in (50, 51, 52, 53): keep_ff(c, s - 50)

            def front_step(c, s):
                if s in (12, 13): scale_x(c, s - 12)
                if s in (18, 20, 22, 24): keep_xi(c, (s - 18) // 2)
                if s in (20, 22, 24, 26): last_tap(c, (s - 20) // 2)
                if s in (27, 28): keep_z(c, s - 27)
                if s in (35, 36): keep_z(c, s - 33)
                if s == 38: silu(c)
                if s == 42: keep_xd(c)
                if s == 43: keep_c(c)
                if s in (47, 49, 54, 56):
                    j = (47, 49, 54, 56).index(s)
                    soft_split(c, j)
                    soft_exp(c, j)
                if s in (48, 50, 55, 57): soft_log(c, (48, 50, 55, 57).index(s))

            for s in range(STEPS):
                front_step((0, 0), s)

            def period(c, parts):
                for s in range(STEPS):
                    if "scan" in parts: decay(c, s)
                    if "end" in parts: end_step(after(c, -2), s, "front" not in parts)
                    if "back" in parts: back_step(after(c, -1), s)
                    if "front" in parts: front_step(after(c, 1), s)
            periods(act, period)

        @block.gpsimd
        def _(pool):
            pool.wait_ge(w_loaded, 16 * 21)
            pool.wait_ge(gn_step, GN_DONE)

            def input_step(c, j):
                wait(pool, sp_step, c, JB * STEPS_SP, STEPS_SP * (j + 1))
                wait(pool, silu_set, c, 2, 1)
                wait(pool, dbu_set, c, NS, 0)
                pool.tensor_tensor(du[:, j, :], delta[:, par(c), j, :], u[:, par(c), j, :],
                                   ALU.mult).then_inc(du_set, 1)

            def times_b(c, n):
                if n == 0:
                    wait(pool, du_set, c, JB, JB)
                wait(pool, bb_in[n % NBB], c, 16 * NS // NBB, 16 * (n // NBB + 1))
                wait(pool, scanned, c, STEPS, 4 * n - 4)
                pool.tensor_tensor(dbu[:, n % 2, :, :], du[:, :, :],
                                   bb[:, n % NBB:n % NBB + 1, :].broadcast_to([P, JB, T]), ALU.mult).then_inc(dbu_set, 1)

            def gate(c, j):
                wait(pool, skip_set, c, JB, j + 1)
                wait(pool, silu_set, c, 2, 2)
                pool.tensor_tensor(u[:, par(c), j, :], u[:, par(c), j, :], sz[:, par(c), j, :],
                                   ALU.mult).then_inc(gated, 1)

            def affine2(c, k):
                wait(pool, nrm_set, c, 3 * Q, 2 * Q)
                wait(pool, affine_step, c, 2, k)
                row = (n2_g, n2_b)[k]
                pool.tensor_tensor(nrm[:, :, :], nrm[:, :, :], row[:, :].unsqueeze(1).broadcast_to([P, Q, DM]),
                                   (ALU.mult, ALU.add)[k]).then_inc(affine_step, 1)

            def residual(c, k):
                wait(pool, xw_in, c, 32, 32)
                wait(pool, rrow_set, c, 1, 1)
                wait(pool, resid_step, c, 3, k)
                v = xw[:, :, :].rearrange("p f (v c) -> p (f v) c", c=CH)
                if k < 2:
                    pool.tensor_tensor(v, v, rrow[:, k * CH:(k + 1) * CH].unsqueeze(1).broadcast_to([P, FB * T // CH, CH]),
                                       (ALU.mult, ALU.add)[k]).then_inc(resid_step, 1)
                else:
                    wait(pool, o_set, c, FB, FB)
                    pool.tensor_tensor(o[:, :, :], o[:, :, :], xw[:, :, :], ALU.add).then_inc(resid_step, 1)

            def end_step(c, n):
                if n == 2: residual(c, 0)
                if n == 3:
                    affine2(c, 0)
                    affine2(c, 1)
                if n == 6: residual(c, 1)
                if n == 10: residual(c, 2)

            def back_step(c, n):
                if n == 5:
                    for j in range(JB):
                        gate(c, j)

            def front_step(c, n):
                if n == 15:
                    for j in range(JB):
                        input_step(c, j)

            front_step((0, 0), NS - 1)

            def period(c, parts):
                for n in range(NS):
                    if "scan" in parts: times_b(c, n)
                    if "end" in parts: end_step(after(c, -2), n)
                    if "back" in parts: back_step(after(c, -1), n)
                    if "front" in parts: front_step(after(c, 1), n)
            periods(pool, period)

        @block.vector
        def _(dve):
            dve.wait_ge(w_loaded, 16 * 21)

            dve.memset(ones[:, :], 1.0).then_inc(prep_dve, 1)
            dve.memset(eps[:, :], EPS).then_inc(prep_dve, 1)
            dve.memset(xd[:, :, :], 1.0).then_inc(prep_dve, 1)
            dve.memset(carry[:, :, :], 0.0).then_inc(prep_dve, 1)
            dve.wait_ge(prep_act, 1)
            dve.tensor_scalar(a_neg[:, :, :], a_neg[:, :, :], -1.0, None, ALU.mult).then_inc(prep_dve, 1)

            def sequence_stats(i):
                for k in range(2):
                    for g in range(8):
                        f, r = g // 4, g % 4
                        wait(dve, seq_turned, (i, k), 8, g + 1)
                        dve.bn_stats(stats[:, f, 2 * i + k, 6 * r:6 * r + 6], ps[:, g, :]).then_inc(seq_stat, 1)
            sequence_stats(0)
            with dve.Fori(1, BATCH // 2) as i:
                sequence_stats(i)
            dve.wait_ge(seq_stat, 8 * BATCH)
            for f in range(FB):
                for b in range(BATCH):
                    dve.bn_aggr(mvs[:, f, b, :], stats[:, f, b, :]).then_inc(gn_aggr, 1)

            def gn_do(ins):
                ins.then_inc(gn_step, 1)
            dve.wait_ge(gn_aggr, FB * BATCH)
            dve.memset(gn[:, :, :], 0.0).then_inc(gn_step, 1)
            dve.wait_ge(gn_step, 1)
            dve.wait_ge(gn_mm, 1)
            dve.tensor_copy(gn[:, 0, :], ps[:, 0, 0:BATCH]).then_inc(gn_step, 1)
            dve.wait_ge(gn_step, 2)
            for f in range(FB):
                dve.tensor_tensor(gn[:, 1 + f, :], mvs[:, f, :, 0], gn[:, 0, :], ALU.subtract)
            dve.tensor_copy(gn[:, 3, :], gn[:, 0, :]).then_inc(gn_step, 1)
            dve.wait_ge(gn_step, 3)
            dve.tensor_tensor(gn[:, 4, :], gn[:, 1, :], gn[:, 1, :], ALU.mult)
            dve.tensor_tensor(gn[:, 5, :], gn[:, 2, :], gn[:, 2, :], ALU.mult).then_inc(gn_step, 1)
            dve.wait_ge(gn_step, 4)
            dve.tensor_tensor(mvs[:, 0, :, 1], mvs[:, 0, :, 1], gn[:, 4, :], ALU.add).then_inc(gn_step, 1)
            dve.tensor_tensor(mvs[:, 1, :, 1], mvs[:, 1, :, 1], gn[:, 5, :], ALU.add).then_inc(gn_step, 1)
            dve.wait_ge(gn_mm, 2)
            dve.wait_ge(gn_step, 6)
            dve.tensor_scalar(gn[:, 2, :], ps[:, 1, 0:BATCH], EPS, None, ALU.add).then_inc(gn_step, 1)
            dve.wait_ge(gn_root, 2)

            def refine(r, v, t, counter, value):
                value(0)
                dve.tensor_tensor(t, r, r, ALU.mult).then_inc(counter, 1)
                value(1)
                dve.scalar_tensor_tensor(out=t, in0=v[0], scalar=v[1], in1=t, op0=ALU.add, op1=ALU.mult).then_inc(counter, 1)
                value(2)
                dve.tensor_scalar(t, t, -0.5, 1.5, ALU.mult, ALU.add).then_inc(counter, 1)
                value(3)
                dve.tensor_tensor(r, r, t, ALU.mult).then_inc(counter, 1)

            refine(gn[:, 1, :], (gn[:, 2, :], 0.0), gn[:, 3, :], gn_step, lambda k: dve.wait_ge(gn_step, GN_V + k))
            dve.wait_ge(gn_step, GN_V + 4)
            pairs = PAIRS // BATCH
            cv = coef[:, :, :].rearrange("p (b k) e -> p b k e", k=pairs)
            for k in range(pairs):
                dve.tensor_copy(cv[:, :, k, 0], gn[:, 1, :])
                dve.scalar_tensor_tensor(out=cv[:, :, k, 1], in0=gn[:, 0, :], scalar=-1.0, in1=gn[:, 1, :],
                                         op0=ALU.mult, op1=ALU.mult)
                last = dve.tensor_scalar(cv[:, :, k, 2], gn[:, 1, :], 1.0, None, ALU.add)
            last.then_inc(gn_step, 1)
            dve.wait_ge(gn_step, GN_DONE)

            def copy(dst, src):
                return dve.tensor_scalar(dst, src, ones[:, 0:1], None, ALU.mult)

            def set_coef(c):
                wait(dve, xn_set, after(c, -1), FB, 0)
                copy(coef_c[:, par(c), 0:3], coef[:, bass.ds(pair_of(c), 1), 0:3]).then_inc(coef_set, 1)

            def set_mask(c):
                wait(dve, ctx_set, c, 1, 0)
                wait(dve, carried, after(c, -1), NS, 0)
                copy(mask[:, 0:1], starts[:, bass.ds(pair_of(after(c, 1)), 1)]).then_inc(mask_set, 1)

            def set_context(c):
                if is_first(c):
                    dve.memset(xi[:, :, 0:KC - 1], 0.0).then_inc(ctx_set, 1)
                    return
                wait(dve, conv_step, c, JB * (KC - 1), 0)
                wait(dve, tap_set, c, JB, 0)
                wait(dve, xi_set, c, JB, 0)
                m = 1.0
                if par(c) == 0:
                    dve.wait_ge(mask_set, pair_of(after(c, -1)) + 1)
                    m = mask[:, 0:1]
                dve.tensor_scalar(xi[:, :, 0:KC - 1], xi[:, :, T:T + KC - 1], m, None, ALU.mult).then_inc(ctx_set, 1)

            def tap(c, j, k):
                base = (KC - 1) * j + KC - 2 - k
                wait(dve, tap_set, c, JB, j + 1)
                wait(dve, ctx_set, c, 1, 1)
                wait(dve, conv_step, c, JB * (KC - 1), base)
                dve.scalar_tensor_tensor(out=v[:, j, :], in0=xi[:, j, k:k + T], scalar=w_cv[:, j, k:k + 1],
                                         in1=v[:, j, :], op0=ALU.mult, op1=ALU.add).then_inc(conv_step, 1)

            def soft(c, j, k):
                wait(dve, sp_step, c, JB * STEPS_SP, STEPS_SP * j + k)
                if k == 0:
                    wait(dve, sp_exp, c, JB, j + 1)
                    ins = dve.tensor_scalar(sp_m[:, :], sp_e[:, j, :], 1.0, 1.0, ALU.add, ALU.subtract)
                if k == 1:
                    wait(dve, sp_log, c, JB, j + 1)
                    ins = dve.tensor_tensor(sp_m[:, :], sp_l[:, j % 2, :], sp_m[:, :], ALU.subtract)
                if k == 2:
                    ins = dve.scalar_tensor_tensor(out=sp_m[:, :], in0=sp_m[:, :], scalar=0.0, in1=sp_e[:, j, :],
                                                   op0=ALU.min, op1=ALU.add)
                if k == 3:
                    wait(dve, sp_relu, c, JB, j + 1)
                    d = delta[:, par(c), j, :]
                    ins = dve.tensor_tensor(d, d, sp_m[:, :], ALU.add)
                ins.then_inc(sp_step, 1)

            def scan(c, s):
                n, j = s // JB, s % JB
                if j == 0:
                    wait(dve, dbu_set, c, NS, n + 1)
                    wait(dve, turned, c, STEPS, 4 * n - 4)
                    wait(dve, carried, c, NS, n - 1)
                wait(dve, da_set, c, STEPS, s + 1)
                dve.tensor_tensor_scan(h[:, n % 2, j, :], ps[:, DA0 + s % 2, :], dbu[:, n % 2, j, :],
                                       carry[:, n, j:j + 1], ALU.mult, ALU.add).then_inc(scanned, 1)

            def keep_state(c, n):
                wait(dve, scanned, c, STEPS, 4 * n + 4)
                m = 1.0
                if par(c) == 1:
                    dve.wait_ge(mask_set, pair_of(c) + 1)
                    m = mask[:, 0:1]
                dve.tensor_scalar(carry[:, n, :], h[:, n % 2, :, T - 1], m, None, ALU.mult).then_inc(carried, 1)

            def add_state(c, n, q):
                wait(dve, turned, c, STEPS, 4 * n + q + 1)
                src, dst = ps[:, HT0 + q % 2, :], y[:, par(c), q, :]
                cn = cs[:, par(c), q, n:n + 1]
                if n == 0:
                    wait(dve, cs_set, c, 1, 1)
                    wait(dve, back_mm, after(c, -2), GB, K_OUT)
                    dve.tensor_scalar(dst, src, cn, None, ALU.mult).then_inc(summed, 1)
                else:
                    wait(dve, summed, c, STEPS, 4 * (n - 1) + q + 1)
                    dve.scalar_tensor_tensor(out=dst, in0=src, scalar=cn, in1=dst, op0=ALU.mult,
                                             op1=ALU.add).then_inc(summed, 1)

            def diag_r(c, k):
                if k == 0:
                    wait(dve, end_mm, c, GE, 0)
                    wait(dve, rdiag_set, c, 3, 0)
                    copy(coef_e[:, 0:3], coef[:, bass.ds(pair_of(c), 1), 0:3]).then_inc(rdiag_set, 1)
                    wait(dve, rdiag_set, c, 3, 1)
                dve.tensor_scalar(rdiag[0:CH, k * CH:(k + 1) * CH], ident[0:CH, 0:CH],
                                  coef_e[0:CH, 2 - k:3 - k], None, ALU.mult).then_inc(rdiag_set, 1)

            def skip(c, j):
                wait(dve, back_mm, c, GB, K_YT + j + 1)
                if j == 0:
                    wait(dve, front_mm, c, GF, G_C + 1)
                    wait(dve, du_set, c, JB, JB)
                w = u[:, par(c), j, :]
                dve.scalar_tensor_tensor(out=w, in0=w, scalar=d_par[:, j:j + 1],
                                         in1=ps[:, BK0 + (K_YT + j) % 2, :],
                                         op0=ALU.mult, op1=ALU.add).then_inc(skip_set, 1)

            def norm_stats(c, k, g):
                base = LN_NORM * k
                if g == 0:
                    wait(dve, ln_step, c, LN_ALL, base)
                if k < 2:
                    wait(dve, back_mm, c, GB, (K_OUT, K_FF2)[k] + g + 1)
                else:
                    wait(dve, affine_step, c, 2, 2)
                for r in range(2):
                    q = 2 * g + r
                    src = nrm[:, q, :] if k == 2 else ps[:, BK0 + ((K_OUT, K_FF2)[k] + g) % 2, r * DM:(r + 1) * DM]
                    dve.bn_stats(st[:, k, q, :], src).then_inc(ln_step, 1)

            def norm_aggr(c, k):
                for q in range(Q):
                    dve.bn_aggr(mv[:, k, q, :], st[:, k, q, :]).then_inc(ln_step, 1)

            def norm_root(c, k):
                base = LN_NORM * k + 2 * Q
                wait(dve, root_step, c, 6, 2 * k + 2)
                refine(rs[:, k, :], (mv[:, k, :, 1], EPS), rt[:, k, :], ln_step,
                       lambda t: wait(dve, ln_step, c, LN_ALL, base + t))
                wait(dve, ln_step, c, LN_ALL, base + 4)
                dve.scalar_tensor_tensor(out=rt[:, k, :], in0=mv[:, k, :, 0], scalar=-1.0, in1=rs[:, k, :],
                                         op0=ALU.mult, op1=ALU.mult).then_inc(ln_step, 1)

            AGGR_AT = {("end", 0): 1, ("end", 19): 2, ("back", 35): 0}

            def before_scan(kind, c, s):
                k = AGGR_AT[(kind, s)]
                wait(dve, ln_step, c, LN_ALL, LN_NORM * k + Q)
                wait(dve, root_step, c, 6, 2 * k)

            def end_step(c, s):
                if ("end", s) in AGGR_AT: norm_aggr(c, AGGR_AT[("end", s)])
                if s == 0:
                    diag_r(c, 0)
                    diag_r(c, 1)
                if s == 4: norm_root(c, 1)
                if s in (17, 18): norm_stats(c, 2, s - 17)
                if s == 23: norm_root(c, 2)

            def back_step(c, s):
                if ("back", s) in AGGR_AT: norm_aggr(c, AGGR_AT[("back", s)])
                if s in (11, 12): skip(c, s - 11)
                if s in (16, 17): skip(c, s - 14)
                if s in (29, 34): norm_stats(c, 0, (s - 29) // 5)
                if s == 38: norm_root(c, 0)
                if s in (59, 61): norm_stats(c, 1, (s - 59) // 2)

            def front_step(c, s):
                if s == 9: set_coef(c)
                if s == 10: set_context(c)
                if s in (22, 24, 26, 28):
                    tap(c, (s - 22) // 2, 2)
                    tap(c, (s - 22) // 2, 1)
                if s in (23, 25, 27, 30): tap(c, (23, 25, 27, 30).index(s), 0)
                if s in (49, 51, 56, 58): soft(c, (49, 51, 56, 58).index(s), 0)
                if s in (50, 52, 57, 59):
                    j = (50, 52, 57, 59).index(s)
                    soft(c, j, 1)
                    soft(c, j, 2)
                    soft(c, j, 3)

            for s in range(STEPS):
                front_step((0, 0), s)

            def period(c, parts):
                if par(c) == 1 and "scan" in parts:
                    set_mask(c)
                for s in range(STEPS):
                    for kind, d in (("end", -2), ("back", -1)):
                        if kind in parts and (kind, s) in AGGR_AT:
                            before_scan(kind, after(c, d), s)
                            if "scan" not in parts:
                                dve.tensor_copy(gn[:, 3, 0:1], gn[:, 0, 0:1])
                    if "scan" in parts: scan(c, s)
                    n, q = s // 4, s % 4
                    if s >= 4 and "scan" in parts:
                        add_state(c, n - 1, q)
                        if q == 0:
                            keep_state(c, n - 1)
                    if s < 4 and "back" in parts:
                        add_state(after(c, -1), NS - 1, q)
                        if q == 0 and "scan" in parts:
                            keep_state(after(c, -1), NS - 1)
                    if "end" in parts: end_step(after(c, -2), s)
                    if "back" in parts: back_step(after(c, -1), s)
                    if "front" in parts: front_step(after(c, 1), s)
            periods(dve, period)


def kernel(**inputs):
    import numpy as np
    import concourse.bacc as bacc
    from concourse import mybir as mb
    from concourse.bass_utils import run_bass_kernel_spmd as run

    def w(name):
        return np.asarray(inputs["L0_conv_" + name])

    def cols(v):
        return v.reshape(-1, P).T

    f = np.arange(P)
    avg = ((f[:, None] % CH) // 2 == (f[None, :] % CH) // 2) / np.float32(8)
    per_seq = PAIRS // BATCH
    inner = (np.arange(PAIRS + 1) % per_seq != 0)[None, :] * np.ones((P, 1))
    consts = np.concatenate([np.eye(P), avg, inner], axis=1).astype(np.float32)

    x_proj = w("x_proj_w").T
    wx = np.zeros((DI, P), x_proj.dtype)
    wx[:, 0:NS] = x_proj[:, R:R + NS]
    wx[:, 96:96 + R] = x_proj[:, 0:R]
    arrays = {
        "x": np.asarray(inputs["x"]), "consts": consts, "win_t": w("in_proj_w").T, "bin_c": cols(w("in_proj_b")),
        "convw": w("conv_w"), "convb": cols(w("conv_b")), "wx": wx, "wc": x_proj[:, R + NS:],
        "wdt": np.concatenate([w("dt_proj_w").T, w("dt_proj_b")[None, :]], axis=0), "alog": w("A_log"),
        "dpar": cols(w("Dp")), "wout": w("out_proj_w").T, "n1g": cols(w("norm1_g")), "n1b": cols(w("norm1_b")),
        "wf1": w("ffn1_w").T, "bf1": cols(w("ffn1_b")), "wf2": w("ffn2_w").T, "bf2": w("ffn2_b"),
        "g2rows": np.tile(w("norm2_g"), (P, 1)), "b2rows": np.tile(w("norm2_b"), (P, 1)),
        "lng": cols(w("ln_g")), "lnb": cols(w("ln_b")),
    }
    nc = bacc.Bacc("TRN2", target_bir_lowering=False, num_devices=1)
    data, args = {}, []
    for name, a in arrays.items():
        a = np.ascontiguousarray(a)
        data[f"in_{name}"] = a
        args.append(nc.dram_tensor(f"in_{name}", a.shape, mb.dt.from_np(a.dtype), kind="ExternalInput").ap())
    args.append(nc.dram_tensor("out_0", (16, 32, 256, 64), mb.dt.float32, kind="ExternalOutput").ap())
    layer_kernel(nc, *args)
    r = run(nc, [data], core_ids=[0])
    return r.results[0]["out_0"]
```

```python
from contextlib import ExitStack

import concourse.bass as bass
from concourse import mybir

F32 = mybir.dt.float32
BF16 = mybir.dt.bfloat16
ALU = mybir.AluOpType
ACT = mybir.ActivationFunctionType

P = 128
DM, DI, DF, NS, R, KC = 256, 512, 512, 16, 16, 4
T = 512
Q = T // P
JB = DI // P
FB = DM // P
MB = DF // P
SEQ, BATCH, CH = 2048, 16, 64
CHUNKS = BATCH * SEQ // T
PAIRS = CHUNKS // 2
STEPS = NS * JB
FIRST_LOOPED = 2
NBB = 2
NDA = 4
LEAD = NDA - 1
NHT = 3
QV = 3
LAG = 6
EPS = 1e-5
LN_SET = "natural_log_exp_and_others"
SILU_SET = "silu_and_others"

HT0, YS0, FR0, BK0 = 0, 3, 4, 6

G_XT, G_XI, G_Z, G_XD, G_C, G_DT = 0, 2, 6, 10, 11, 12
GF = 16
K_YT, K_OUT, K_N1T, K_FF1, K_FF2 = 0, 4, 6, 8, 12
GB = 14
E_R, E_N3T = 0, 1
GE = 3
LN_NORM, LN_ALL = 13, 39
STEPS_SP = 4
GN_DEV, GN_VAR, GN_V, GN_DONE = 1, 6, 7, 12


def layer_kernel(nc, x, consts, win_t, bin_c, convw, convb, wx, wc, wdt, alog, dpar, wout, n1g, n1b,
                 wf1, bf1, wf2, bf2, g2rows, b2rows, lng, lnb, out):
    x_tok = x.rearrange("b v (w r) c -> (b v w) (r c)", r=DM // CH).rearrange(
        "(c q p) f -> c p q f", p=P, q=Q)
    x_nat = x.rearrange("b (k v) (f w) c -> (b k) f w v c", k=SEQ // T, f=FB)
    o_nat = out.rearrange("b (k v) (f w) c -> (b k) f w v c", k=SEQ // T, f=FB)
    x_seq = x.rearrange("b v (w r) c -> b (v w) (r c)", r=DM // CH).rearrange(
        "b (q p) f -> b p q f", p=P)

    with ExitStack() as ctx:
        def sb(name, shape, dt=F32):
            return ctx.enter_context(nc.sbuf_tensor(name, shape, dt))

        def sem(name):
            return ctx.enter_context(nc.semaphore(name))

        ps = ctx.enter_context(nc.psum_tensor("ps", [P, 8, 512], F32))

        cst = sb("cst", [P, 2 * P + PAIRS + 1])
        ident = cst[:, 0:P]
        group_avg = cst[:, P:2 * P]
        starts = cst[:, 2 * P:]
        mask = sb("mask", [P, 2])
        w_in = sb("w_in", [P, FB, 2 * DI])
        b_in = sb("b_in", [P, 2 * JB])
        w_cv = sb("w_cv", [P, JB, KC])
        b_cv = sb("b_cv", [P, JB])
        w_x = sb("w_x", [P, JB, 96 + R])
        w_c = sb("w_c", [P, JB, NS])
        w_dt = sb("w_dt", [P, DI])
        b_f2 = w_dt[0:1, 0:DM]
        ones = w_dt[0:CH, DM:DM + P]
        rdiag = w_dt[0:CH, DM + P:DM + P + 2 * CH]
        a_neg = sb("a_neg", [P, JB, NS])
        d_par = sb("d_par", [P, JB])
        w_out = sb("w_out", [P, JB, DM])
        n1_g = sb("n1_g", [P, FB])
        n1_b = sb("n1_b", [P, FB])
        w_f1 = sb("w_f1", [P, FB, DF])
        b_f1 = sb("b_f1", [P, MB])
        w_f2 = sb("w_f2", [P, MB, DM])
        n2_g = sb("n2_g", [P, DM])
        n2_b = sb("n2_b", [P, DM])
        ln_g = sb("ln_g", [P, FB])
        ln_b = sb("ln_b", [P, FB])

        xt = sb("xt", [P, Q, DM])
        coef = sb("coef", [P, PAIRS, 4])
        coef_c = sb("coef_c", [P, 2, 4])
        coef_e = sb("coef_e", [P, 4])
        xn = sb("xn", [P, 2, FB, T])
        xi = sb("xi", [P, JB, KC - 1 + T])
        u = sb("u", [P, 2, JB, T])
        sz = sb("sz", [P, 2, JB, T])
        v = sb("v", [P, JB, T])
        xd = sb("xd", [P, 2, T])
        cs = sb("cs", [P, 2, Q, NS])
        sp_e = v
        sp_m = sb("sp_m", [P, T])
        delta = sb("delta", [P, 2, JB, T])
        du = sb("du", [P, JB, T])
        bb = sb("bb", [P, NBB, T])
        dbu = sb("dbu", [P, 2, JB, T])
        h = sb("h", [P, 2, JB, T])
        da = sb("da", [P, NDA, T])
        hs = sb("hs", [P, 2, DI])
        carry = sb("carry", [P, NS, JB])
        y = sb("y", [P, 2, Q, DI])
        xres = sb("xres", [P, FB, T])
        st = sb("st", [P, 3, Q, 6])
        mv = sb("mv", [P, 3, Q, 2])
        rs = sb("rs", [P, 3, Q])
        rt = sb("rt", [P, 3, Q])
        eps = sb("eps", [P, 3])
        nrm = sb("nrm", [P, Q, DM])
        h1 = sb("h1", [P, FB, T])
        ff = sb("ff", [P, MB, T])
        rrow = group_avg
        xw = sb("xw", [P, FB, T])
        sp_l = xw
        o = xt[:, :, :].rearrange("p (f a) d -> p f (a d)", f=FB)
        stats = du[:, :, :].rearrange("p j t -> p (j t)")[:, 0:FB * BATCH * 24].rearrange(
            "p (f b s) -> p f b s", f=FB, b=BATCH)
        seq_buf = [u[:, :, :, :].rearrange("p a j t -> p (a j t)").rearrange("p (q f) -> p q f", f=DM),
                   sz[:, :, :, :].rearrange("p a j t -> p (a j t)").rearrange("p (q f) -> p q f", f=DM)]
        mvs = h[:, 0, 0, 0:FB * BATCH * 2].rearrange("p (f b e) -> p f b e", f=FB, e=2)
        gn = h[:, 0, 1, 0:6 * BATCH].rearrange("p (k b) -> p k b", b=BATCH)

        w_loaded = sem("w_loaded")
        seq_in = [sem("seq_in0"), sem("seq_in1")]
        seq_turned, seq_stat = sem("seq_turned"), sem("seq_stat")
        gn_aggr, gn_step, gn_mm, gn_root = sem("gn_aggr"), sem("gn_step"), sem("gn_mm"), sem("gn_root")
        prep_act, prep_dve = sem("prep_act"), sem("prep_dve")
        x_in, xw_in, stored = sem("x_in"), sem("xw_in"), sem("stored")
        front_mm, back_mm, end_mm = sem("front_mm"), sem("back_mm"), sem("end_mm")
        coef_set, ctx_set, mask_set = sem("coef_set"), sem("ctx_set"), sem("mask_set")
        xn_set, xi_set, tap_set, conv_step, z_set, silu_set = (
            sem(n) for n in ("xn_set", "xi_set", "tap_set", "conv_step", "z_set", "silu_set"))
        xd_set, cs_set, xres_set, nrm_set = sem("xd_set"), sem("cs_set"), sem("xres_set"), sem("nrm_set")
        sp_abs, sp_relu, sp_exp, sp_log, sp_step = (sem(n) for n in ("sp_abs", "sp_relu", "sp_exp", "sp_log", "sp_step"))
        bb_in = [sem(f"bb_in{k}") for k in range(NBB)]
        du_set, dbu_set = sem("du_set"), sem("dbu_set")
        da_set, scanned, carried, turned, summed = (sem(n) for n in ("da_set", "scanned", "carried", "turned", "summed"))
        scaled, y_summed, y_set = sem("scaled"), sem("y_summed"), sem("y_set")
        rdiag_set, rrow_set, skip_set, gated = sem("rdiag_set"), sem("rrow_set"), sem("skip_set"), sem("gated")
        ln_step, root_step, h1_set, ff_set, affine_step, o_set, resid_step = (
            sem(n) for n in ("ln_step", "root_step", "h1_set", "ff_set", "affine_step", "o_set", "resid_step"))

        block = ctx.enter_context(nc.Block())

        def wait(eng, s, c, per, n):
            i, k = c
            if isinstance(i, int):
                v = (2 * i + k) * per + n
                if v > 0:
                    eng.wait_ge(s, v)
            else:
                assert 2 * FIRST_LOOPED * per + k * per + n > 0
                eng.wait_ge(s, i * (2 * per) + (k * per + n))

        def wait_both(eng, a, b):
            values = []
            for s, (i, k), per, n in (a, b):
                assert 2 * FIRST_LOOPED * per + k * per + n > 0 or isinstance(i, int)
                v = i * (2 * per) + (k * per + n)
                values.append((s, v if isinstance(i, int) else eng.to_reg(v)))
            for s, v in values:
                if not isinstance(v, int) or v > 0:
                    eng.wait_ge(s, v)

        def after(c, d):
            return (c[0], c[1] + d)

        def par(c):
            return c[1] % 2

        def pair_of(c):
            i, k = c
            return i + k // 2

        def exists(c):
            return not isinstance(c[0], int) or 0 <= 2 * c[0] + c[1] < CHUNKS

        def is_first(c):
            return isinstance(c[0], int) and 2 * c[0] + c[1] == 0

        def periods(eng, period):
            every = ("scan", "front", "back", "end")
            period((0, 0), ("scan", "front"))
            period((0, 1), ("scan", "front", "back"))
            period((1, 0), every)
            period((1, 1), every)
            with eng.Fori(FIRST_LOOPED, PAIRS - 1) as i:
                period((i, 0), every)
                period((i, 1), every)
            period((PAIRS - 1, 0), every)
            period((PAIRS - 1, 1), ("scan", "back", "end"))
            period((PAIRS - 1, 2), ("back", "end"))
            period((PAIRS - 1, 3), ("end",))

        def turned_bank(n, q):
            return ps[:, HT0 + (JB * n + q) % NHT, :]

        @block.sync
        def _(sp):
            for dst, src in (
                    (cst[:, :], consts), (w_in[:, :, :], win_t.rearrange("(f p) e -> p f e", p=P)),
                    (b_in[:, :], bin_c),
                    (w_cv[:, :, :], convw.rearrange("(j p) k -> p j k", p=P)),
                    (b_cv[:, :], convb),
                    (w_x[:, :, :], wx.rearrange("(j p) m -> p j m", p=P)),
                    (w_c[:, :, :], wc.rearrange("(j p) m -> p j m", p=P)),
                    (w_dt[96:96 + R + 1, :], wdt),
                    (a_neg[:, :, :], alog.rearrange("(j p) n -> p j n", p=P)),
                    (d_par[:, :], dpar),
                    (w_out[:, :, :], wout.rearrange("(j p) m -> p j m", p=P)),
                    (n1_g[:, :], n1g),
                    (n1_b[:, :], n1b),
                    (w_f1[:, :, :], wf1.rearrange("(f p) m -> p f m", p=P)),
                    (b_f1[:, :], bf1),
                    (w_f2[:, :, :], wf2.rearrange("(j p) m -> p j m", p=P)),
                    (b_f2, bf2.rearrange("(a m) -> a m", a=1)),
                    (n2_g[:, :], g2rows), (n2_b[:, :], b2rows),
                    (ln_g[:, :], lng),
                    (ln_b[:, :], lnb)):
                sp.dma_start(dst, src).then_inc(w_loaded, 16)

            def load_sequences(i):
                for k in range(2):
                    wait(sp, seq_turned, (i, k), 8, -8)
                    sp.dma_start(seq_buf[k], x_seq[2 * i + k]).then_inc(seq_in[k], 16)
            load_sequences(0)
            with sp.Fori(1, BATCH // 2) as i:
                load_sequences(i)

            def load_x(c):
                wait_both(sp, (front_mm, after(c, -1), GF, G_XI),
                          (stored, after(c, -3), 32, 0))
                i, k = c
                sp.dma_start(xt[:, :, :], x_tok[2 * i + k]).then_inc(x_in, 16)

            def load_residual(c):
                i, k = c
                if exists(after(c, 2)):
                    wait(sp, sp_step, after(c, 2), JB * STEPS_SP, JB * STEPS_SP)
                else:
                    wait(sp, resid_step, c, 3, 0)
                for f in range(FB):
                    sp.dma_start(xw[:, f, :].rearrange("p (v c) -> p v c", c=CH),
                                 x_nat[2 * i + k, f]).then_inc(xw_in, 16)

            def store(c):
                i, k = c
                wait(sp, resid_step, c, 3, 3)
                for f in range(FB):
                    sp.dma_start(o_nat[2 * i + k, f],
                                 o[:, f, :].rearrange("p (v c) -> p v c", c=CH)).then_inc(stored, 16)

            def spread_b(c, n):
                used = (dbu_set, c, NS, n - NBB + 1)
                if n == 0:
                    wait_both(sp, (xd_set, c, 1, 1), used)
                else:
                    wait(sp, *used)
                sp.dma_start(bb[:, n % NBB, :], xd[n:n + 1, par(c), :].unsqueeze(1).broadcast_to([1, P, T])).then_inc(bb_in[n % NBB], 16)

            load_x((0, 0))
            load_x((0, 1))
            for n in range(NBB - 1):
                spread_b((0, 0), n)

            def period(c, parts):
                for n in range(NS):
                    if "scan" in parts and n + NBB - 1 < NS:
                        spread_b(c, n + NBB - 1)
                    if n == 12 and exists(after(c, 2)):
                        load_x(after(c, 2))
                    if "front" in parts and n + NBB - 1 >= NS:
                        spread_b(after(c, 1), n + NBB - 1 - NS)
                    if "end" in parts and n == 1: load_residual(after(c, -2))
                    if "end" in parts and n == 10: store(after(c, -2))
            periods(sp, period)
            sp.wait_ge(stored, 32 * CHUNKS)

        FRONT_ORDER = ([("end", E_R)] + [("front", k) for k in range(G_XD)] + [("end", E_N3T), ("end", E_N3T + 1)]
                       + [("front", k) for k in range(G_XD, GF)])

        def front_bank(g):
            return FR0 + FRONT_ORDER.index(g) % 2

        @block.tensor
        def _(pe):
            pe.wait_ge(w_loaded, 16 * 21)

            def turn_sequences(i):
                for k in range(2):
                    wait(pe, seq_in[k], (i, 0), 8, 16)
                    for g in range(8):
                        f, r = g // 4, g % 4
                        wait(pe, seq_stat, (i, k), 8, g - 7)
                        for t in range(4):
                            mm = pe.transpose(ps[:, g, t * P:(t + 1) * P],
                                              seq_buf[k][:, 4 * r + t, f * P:(f + 1) * P], ident)
                        mm.then_inc(seq_turned, 1)
            turn_sequences(0)
            with pe.Fori(1, BATCH // 2) as i:
                turn_sequences(i)

            def average(src, bank, value):
                pe.wait_ge(gn_step, value)
                for f in range(FB):
                    mm = pe.matmul(ps[:, bank, 0:BATCH], group_avg, src(f), start=(f == 0), stop=(f == FB - 1))
                mm.then_inc(gn_mm, 1)
            pe.wait_ge(gn_aggr, FB * BATCH)
            pe.wait_ge(seq_stat, 8 * BATCH)
            average(lambda f: mvs[:, f, :, 0], 0, GN_DEV)
            average(lambda f: mvs[:, f, :, 1], 1, GN_VAR)
            pe.wait_ge(prep_dve, 6)

            def front_read(k, c):
                if k < G_XI:
                    wait(pe, xn_set, c, FB, k + 1)
                elif k < G_Z:
                    wait(pe, xi_set, c, JB, k - G_XI + 1)
                elif k < G_XD:
                    wait(pe, z_set, c, JB, k - G_Z + 1)
                elif k == G_XD:
                    wait(pe, xd_set, c, 1, 1)
                elif k == G_C:
                    wait(pe, cs_set, c, 1, 1)
                else:
                    wait(pe, sp_abs, c, JB, k - G_DT + 1)
                    wait(pe, sp_relu, c, JB, k - G_DT + 1)

            def end_read(k, c):
                if k == E_R:
                    wait(pe, rrow_set, c, 1, 1)
                else:
                    wait(pe, o_set, c, FB, k - E_N3T + 1)

            def front_free(g, c):
                at = FRONT_ORDER.index(g)
                users = [(x, 0) for x in FRONT_ORDER[:at]][::-1] + [(x, -1) for x in FRONT_ORDER[::-1]]
                for x, d in users:
                    kind, k = x
                    chunk = after(c, d + (1 if kind == "front" else -2))
                    if front_bank(x) == front_bank(g) and exists(chunk):
                        (front_read if kind == "front" else end_read)(k, chunk)
                        return

            def bank(kind, k):
                return ps[:, front_bank((kind, k)), :]

            def turn_x(c, f):
                if f == 0:
                    wait(pe, x_in, c, 16, 16)
                front_free(("front", G_XT + f), after(c, -1))
                for q in range(Q):
                    mm = pe.transpose(bank("front", G_XT + f)[:, q * P:(q + 1) * P], xt[:, q, f * P:(f + 1) * P], ident)
                mm.then_inc(front_mm, 1)

            def in_proj(c, j):
                g = G_XI + j
                if j == 0:
                    wait(pe, xn_set, c, FB, FB)
                front_free(("front", g), after(c, -1))
                for f in range(FB):
                    mm = pe.matmul(bank("front", g), w_in[:, f, j * P:(j + 1) * P], xn[:, par(c), f, :],
                                   start=(f == 0), stop=(f == FB - 1))
                mm.then_inc(front_mm, 1)

            def x_proj(c, part):
                if part == 0:
                    wait(pe, silu_set, c, 2, 1)
                    front_free(("front", G_XD), after(c, -1))
                for j in (2 * part, 2 * part + 1):
                    mm = pe.matmul(bank("front", G_XD)[0:96 + R, :], w_x[:, j, :], u[:, par(c), j, :],
                                   start=(j == 0), stop=(j == JB - 1))
                if part == 1:
                    mm.then_inc(front_mm, 1)

            def c_proj(c):
                front_free(("front", G_C), after(c, -1))
                for q in range(Q):
                    for j in range(JB):
                        mm = pe.matmul(bank("front", G_C)[:, q * NS:(q + 1) * NS], u[:, par(c), j, q * P:(q + 1) * P],
                                       w_c[:, j, :], start=(j == 0), stop=(j == JB - 1))
                mm.then_inc(front_mm, 1)

            def dt_proj(c, j):
                if j == 0:
                    wait(pe, xd_set, c, 1, 1)
                front_free(("front", G_DT + j), after(c, -1))
                pe.matmul(bank("front", G_DT + j), w_dt[96:96 + R + 1, j * P:(j + 1) * P],
                          xd[96:96 + R + 1, par(c), :], start=True, stop=True).then_inc(front_mm, 1)

            def turn_h(c, n, q):
                if q == 0:
                    wait(pe, scanned, c, STEPS, 4 * n + 4)
                k = Q * n + q - NHT
                last = c
                if k < 0:
                    k = max(m for m in range(STEPS) if m % NHT == (Q * n + q) % NHT)
                    last = after(c, -1)
                if k % Q < QV:
                    wait(pe, summed, last, NS * QV, QV * (k // Q) + k % Q + 1)
                else:
                    wait(pe, scaled, last, NS, k // Q + 1)
                for j in range(JB):
                    mm = pe.transpose(turned_bank(n, q)[:, j * P:(j + 1) * P], h[:, n % 2, j, q * P:(q + 1) * P], ident)
                mm.then_inc(turned, 1)

            def sum_last_tile(c, n):
                wait(pe, scaled, c, NS, n + 1)
                if n == 0:
                    wait(pe, y_set, c, 1, 0)
                pe.matmul(ps[:, YS0, :], ident, hs[:, n % 2, :], start=(n == 0), stop=(n == NS - 1)
                          ).then_inc(y_summed, 1)

            def back_bank(k):
                return ps[:, BK0 + k % 2, :]

            def back_free(k, c):
                k, c = (k - 2, c) if k >= 2 else (k - 2 + GB, after(c, -1))
                if k < K_OUT:
                    wait(pe, skip_set, c, JB, k - K_YT + 1)
                elif k < K_N1T:
                    wait(pe, nrm_set, c, 3 * Q, 2 * (k - K_OUT + 1))
                elif k < K_FF1:
                    wait(pe, h1_set, c, FB, k - K_N1T + 1)
                elif k < K_FF2:
                    wait(pe, ff_set, c, MB, k - K_FF1 + 1)
                else:
                    wait(pe, nrm_set, c, 3 * Q, Q + 2 * (k - K_FF2 + 1))

            def turn_y(c, j):
                wait(pe, summed, c, NS * QV, NS * QV)
                wait(pe, y_set, c, 1, 1)
                back_free(K_YT + j, c)
                for q in range(Q):
                    mm = pe.transpose(back_bank(K_YT + j)[:, q * P:(q + 1) * P], y[:, par(c), q, j * P:(j + 1) * P],
                                      ident)
                mm.then_inc(back_mm, 1)

            def out_proj(c, q):
                g, r = q // 2, q % 2
                if r == 0:
                    wait(pe, gated, c, JB, JB)
                    wait(pe, xres_set, c, FB, FB)
                    back_free(K_OUT + g, c)
                dst = back_bank(K_OUT + g)
                for j in range(JB):
                    pe.matmul(dst[:, r * DM:(r + 1) * DM], u[:, par(c), j, q * P:(q + 1) * P], w_out[:, j, :],
                              start=(j == 0), stop=False)
                for f in range(FB):
                    mm = pe.matmul(dst[:, r * DM + f * P:r * DM + (f + 1) * P], xres[:, f, q * P:(q + 1) * P], ident,
                                   start=False, stop=(f == FB - 1))
                if r == 1:
                    mm.then_inc(back_mm, 1)

            def turn_norm(c, f):
                wait(pe, nrm_set, c, 3 * Q, Q)
                back_free(K_N1T + f, c)
                for q in range(Q):
                    mm = pe.transpose(back_bank(K_N1T + f)[:, q * P:(q + 1) * P], nrm[:, q, f * P:(f + 1) * P], ident)
                mm.then_inc(back_mm, 1)

            def ffn1(c, m):
                wait(pe, h1_set, c, FB, FB)
                back_free(K_FF1 + m, c)
                for f in range(FB):
                    mm = pe.matmul(back_bank(K_FF1 + m), w_f1[:, f, m * P:(m + 1) * P], h1[:, f, :],
                                   start=(f == 0), stop=(f == FB - 1))
                mm.then_inc(back_mm, 1)

            def ffn2(c, q):
                g, r = q // 2, q % 2
                if r == 0:
                    wait(pe, ff_set, c, MB, MB)
                    back_free(K_FF2 + g, c)
                dst = back_bank(K_FF2 + g)
                for m in range(MB):
                    pe.matmul(dst[:, r * DM:(r + 1) * DM], ff[:, m, q * P:(q + 1) * P], w_f2[:, m, :],
                              start=(m == 0), stop=False)
                pe.matmul(dst[:, r * DM:(r + 1) * DM], ones[0:1, :], b_f2, start=False, stop=False)
                for f in range(FB):
                    mm = pe.matmul(dst[:, r * DM + f * P:r * DM + (f + 1) * P], h1[:, f, q * P:(q + 1) * P], ident,
                                   start=False, stop=(f == FB - 1))
                if r == 1:
                    mm.then_inc(back_mm, 1)

            def spread_r(c):
                wait(pe, rdiag_set, c, 3, 3)
                front_free(("end", E_R), after(c, 2))
                pe.matmul(bank("end", E_R)[:, 0:2 * CH], ones, rdiag,
                          start=True, stop=True).then_inc(end_mm, 1)

            def turn_last(c, f):
                wait(pe, nrm_set, c, 3 * Q, 3 * Q)
                front_free(("end", E_N3T + f), after(c, 2))
                for q in range(Q):
                    mm = pe.transpose(bank("end", E_N3T + f)[:, q * P:(q + 1) * P], nrm[:, q, f * P:(f + 1) * P], ident)
                mm.then_inc(end_mm, 1)

            def end_step(c, s):
                if s == 1: spread_r(c)
                if s in (29, 30): turn_last(c, s - 29)

            def back_step(c, s):
                if s in (10, 11): turn_y(c, s - 10)
                if s in (15, 16): turn_y(c, 2 + s - 15)
                if s in (26, 28, 31, 33): out_proj(c, (26, 28, 31, 33).index(s))
                if s in (44, 45): turn_norm(c, s - 44)
                if s in (48, 50, 52, 54): ffn1(c, (s - 48) // 2)
                if s in (57, 59, 61, 63): ffn2(c, (s - 57) // 2)

            def front_step(c, s):
                if s in (4, 5): turn_x(c, s - 4)
                if s in (11, 13, 17, 19): in_proj(c, (11, 13, 17, 19).index(s))
                if s in (21, 22, 24, 25): in_proj(c, JB + (21, 22, 24, 25).index(s))
                if s in (37, 38): x_proj(c, s - 37)
                if s == 39: c_proj(c)
                if s in (42, 43, 46, 48): dt_proj(c, (42, 43, 46, 48).index(s))

            for s in range(STEPS):
                front_step((0, 0), s)

            def period(c, parts):
                for s in range(STEPS):
                    if s >= 4 and "scan" in parts:
                        turn_h(c, s // 4 - 1, s % 4)
                    if s < 4 and "back" in parts:
                        turn_h(after(c, -1), NS - 1, s)
                    n = (s - 11) // 4
                    if s % 4 == 3 and n >= 0 and "scan" in parts:
                        sum_last_tile(c, n)
                    if s % 4 == 3 and n < 0 and "back" in parts:
                        sum_last_tile(after(c, -1), NS + n)
                    if "end" in parts: end_step(after(c, -2), s)
                    if "back" in parts: back_step(after(c, -1), s)
                    if "front" in parts: front_step(after(c, 1), s)
            periods(pe, period)

        @block.scalar
        def _(act):
            nc.scalar.preload_act_table_set(LN_SET)
            act.wait_ge(w_loaded, 16 * 21)
            act.activation(a_neg[:, :, :], a_neg[:, :, :], ACT.Exp).then_inc(prep_act, 1)
            act.wait_ge(prep_dve, 6)
            act.wait_ge(gn_step, GN_V)
            act.activation(gn[:, 3, :], gn[:, 2, :], ACT.Ln).then_inc(gn_root, 1)
            act.wait_ge(gn_root, 1)
            act.activation(gn[:, 1, :], gn[:, 3, :], ACT.Exp, scale=-0.5).then_inc(gn_root, 1)
            act.wait_ge(gn_step, GN_DONE)

            def bank(kind, k):
                return ps[:, front_bank((kind, k)), :]

            def back_bank(k):
                return ps[:, BK0 + k % 2, :]

            def scale_x(c, f):
                wait(act, front_mm, c, GF, G_XT + f + 1)
                wait(act, coef_set, c, 1, 1)
                wait(act, xres_set, after(c, -2), FB, FB)
                k = coef_c[:, par(c), :]
                act.activation(xn[:, par(c), f, :], bank("front", G_XT + f), ACT.Identity,
                               scale=k[:, 0:1], bias=k[:, 1:2]).then_inc(xn_set, 1)

            def keep_xres(c, f):
                wait(act, back_mm, after(c, -1), GB, K_N1T)
                wait(act, xn_set, c, FB, FB)
                act.activation(xres[:, f, :], xn[:, par(c), f, :], ACT.Identity).then_inc(xres_set, 1)

            def keep_xi(c, j):
                wait(act, front_mm, c, GF, G_XI + j + 1)
                wait(act, ctx_set, c, 1, 1)
                act.activation(xi[:, j, KC - 1:], bank("front", G_XI + j), ACT.Identity,
                               bias=b_in[:, j:j + 1]).then_inc(xi_set, 1)

            def last_tap(c, j):
                wait(act, xi_set, c, JB, j + 1)
                wait(act, sp_step, c, JB * STEPS_SP, 0)
                act.activation(v[:, j, :], xi[:, j, KC - 1:], ACT.Identity, scale=w_cv[:, j, KC - 1:KC],
                               bias=b_cv[:, j:j + 1]).then_inc(tap_set, 1)

            def keep_z(c, j):
                wait(act, front_mm, c, GF, G_Z + j + 1)
                wait(act, gated, after(c, -2), JB, JB)
                act.activation(sz[:, par(c), j, :], bank("front", G_Z + j), ACT.Identity,
                               bias=b_in[:, JB + j:JB + j + 1]).then_inc(z_set, 1)

            def silu_u(c):
                nc.scalar.preload_act_table_set(SILU_SET)
                wait(act, conv_step, c, JB * (KC - 1), JB * (KC - 1))
                wait(act, back_mm, after(c, -2), GB, K_N1T)
                act.activation(u[:, par(c), :, :], v[:, :, :], ACT.Silu).then_inc(silu_set, 1)
                nc.scalar.preload_act_table_set(LN_SET)

            def silu_z(c):
                nc.scalar.preload_act_table_set(SILU_SET)
                wait(act, z_set, c, JB, JB)
                act.activation(sz[:, par(c), :, :], sz[:, par(c), :, :], ACT.Silu).then_inc(silu_set, 1)
                nc.scalar.preload_act_table_set(LN_SET)

            def keep_xd(c):
                wait(act, front_mm, c, GF, G_XD + 1)
                wait(act, dbu_set, after(c, -1), NS, 0)
                act.activation(xd[0:96 + R, par(c), :], bank("front", G_XD)[0:96 + R, :], ACT.Identity
                               ).then_inc(xd_set, 1)

            def keep_c(c):
                wait(act, front_mm, c, GF, G_C + 1)
                wait(act, summed, after(c, -2), NS * QV, NS * QV)
                wait(act, scaled, after(c, -2), NS, NS)
                act.activation(cs[:, par(c), :, :], bank("front", G_C)[:, 0:Q * NS], ACT.Identity).then_inc(cs_set, 1)

            def soft_split(c, j):
                wait(act, front_mm, c, GF, G_DT + j + 1)
                wait(act, silu_set, c, 2, 1)
                act.activation(sp_e[:, j, :], bank("front", G_DT + j), ACT.Abs).then_inc(sp_abs, 1)
                wait(act, da_set, after(c, -1), STEPS, 0)
                wait(act, du_set, after(c, -1), JB, 0)
                act.activation(delta[:, par(c), j, :], bank("front", G_DT + j), ACT.Relu).then_inc(sp_relu, 1)

            def soft_exp(c, j):
                wait(act, sp_abs, c, JB, j + 1)
                act.activation(sp_e[:, j, :], sp_e[:, j, :], ACT.Exp, scale=-1.0).then_inc(sp_exp, 1)

            def soft_log(c, j):
                wait(act, sp_exp, c, JB, j + 1)
                wait(act, sp_step, c, JB * STEPS_SP, STEPS_SP * (j - 1) - 2)
                wait(act, resid_step, after(c, -3), 3, 3)
                act.activation(sp_l[:, j % 2, :], sp_e[:, j, :], ACT.Ln, bias=1.0).then_inc(sp_log, 1)

            def decay(c, s):
                n, j = s // JB, s % JB
                if s == 0:
                    wait(act, sp_step, c, JB * STEPS_SP, JB * STEPS_SP)
                wait(act, scanned, c, STEPS, s - NDA + 1)
                act.activation(da[:, s % NDA, :], delta[:, par(c), j, :], ACT.Exp,
                               scale=a_neg[:, j, n:n + 1]).then_inc(da_set, 1)

            def scale_last_tile(c, n):
                wait(act, turned, c, STEPS, 4 * n + Q)
                wait(act, y_summed, c, NS, n - 1)
                if n == 0:
                    wait(act, cs_set, c, 1, 1)
                act.activation(hs[:, n % 2, :], turned_bank(n, Q - 1), ACT.Identity,
                               scale=cs[:, par(c), Q - 1, n:n + 1]).then_inc(scaled, 1)

            def keep_y(c):
                wait(act, y_summed, c, NS, NS)
                wait(act, back_mm, after(c, -2), GB, K_OUT)
                act.activation(y[:, par(c), Q - 1, :], ps[:, YS0, :], ACT.Identity).then_inc(y_set, 1)

            def root(c, k):
                wait(act, ln_step, c, LN_ALL, LN_NORM * k + 2 * Q)
                wait(act, nrm_set, c, 3 * Q, Q * k)
                act.activation(rs[:, k, :], mv[:, k, :, 1], ACT.Ln, bias=eps[:, 0:1]).then_inc(root_step, 1)
                wait(act, root_step, c, 6, 2 * k + 1)
                act.activation(rs[:, k, :], rs[:, k, :], ACT.Exp, scale=-0.5).then_inc(root_step, 1)

            def norm(c, k, g):
                wait(act, ln_step, c, LN_ALL, LN_NORM * (k + 1))
                if k == 0:
                    wait(act, end_mm, after(c, -1), GE, GE)
                if k == 1:
                    wait(act, back_mm, c, GB, K_FF1)
                for r in range(2):
                    q = 2 * g + r
                    src = nrm[:, q, :] if k == 2 else back_bank((K_OUT, K_FF2)[k] + g)[:, r * DM:(r + 1) * DM]
                    act.activation(nrm[:, q, :], src, ACT.Identity, scale=rs[:, k, q:q + 1],
                                   bias=rt[:, k, q:q + 1]).then_inc(nrm_set, 1)

            def keep_h1(c, f):
                wait(act, back_mm, c, GB, K_N1T + f + 1)
                wait(act, back_mm, after(c, -1), GB, GB)
                act.activation(h1[:, f, :], back_bank(K_N1T + f), ACT.Identity, scale=n1_g[:, f:f + 1],
                               bias=n1_b[:, f:f + 1]).then_inc(h1_set, 1)

            def keep_ff(c, m):
                wait(act, back_mm, c, GB, K_FF1 + m + 1)
                act.activation(ff[:, m, :], back_bank(K_FF1 + m), ACT.Relu, bias=b_f1[:, m:m + 1]).then_inc(ff_set, 1)

            def keep_r(c):
                wait(act, end_mm, c, GE, E_R + 1)
                wait(act, resid_step, c, 3, 0)
                act.activation(rrow[:, :], bank("end", E_R)[:, 0:2 * CH], ACT.Identity).then_inc(rrow_set, 1)

            def keep_o(c, f, last):
                wait(act, end_mm, c, GE, E_N3T + f + 1)
                if last:
                    act.wait_ge(front_mm, GF * CHUNKS)
                    wait(act, stored, c, 32, 0)
                else:
                    wait(act, front_mm, after(c, 3), GF, G_XI)
                act.activation(o[:, f, :], bank("end", E_N3T + f), ACT.Identity, scale=ln_g[:, f:f + 1],
                               bias=ln_b[:, f:f + 1]).then_inc(o_set, 1)

            def end_step(c, s, last):
                if s == 2: keep_r(c)
                if s == 5: root(c, 1)
                if s in (8, 9): norm(c, 1, s - 8)
                if s == 21: root(c, 2)
                if s in (25, 26): norm(c, 2, s - 25)
                if s in (31, 32): keep_o(c, s - 31, last)

            def back_step(c, s):
                if s in (0, 1): keep_xres(c, s)
                if s == 38: root(c, 0)
                if s in (41, 42): norm(c, 0, s - 41)
                if s in (46, 47): keep_h1(c, s - 46)
                if s in (50, 52, 54, 56): keep_ff(c, (s - 50) // 2)

            def front_step(c, s):
                if s in (6, 7): scale_x(c, s - 6)
                if s in (13, 15, 19, 21): keep_xi(c, (13, 15, 19, 21).index(s))
                if s in (14, 16, 20, 22): last_tap(c, (14, 16, 20, 22).index(s))
                if s in (23, 24, 26, 27): keep_z(c, (23, 24, 26, 27).index(s))
                if s == 35: silu_u(c)
                if s == 57: silu_z(c)
                if s == 40: keep_xd(c)
                if s == 41: keep_c(c)
                if s in (44, 46, 48, 50):
                    j = (44, 46, 48, 50).index(s)
                    soft_split(c, j)
                    soft_exp(c, j)
                if s in (45, 47, 49, 51): soft_log(c, (45, 47, 49, 51).index(s))

            for s in range(STEPS):
                front_step((0, 0), s)
            for s in range(LEAD):
                decay((0, 0), s)

            def period(c, parts):
                for s in range(STEPS):
                    if s + LEAD < STEPS and "scan" in parts: decay(c, s + LEAD)
                    if s + LEAD >= STEPS and "front" in parts: decay(after(c, 1), s + LEAD - STEPS)
                    n = (s - 9) // 4
                    if s % 4 == 1 and n >= 0 and "scan" in parts:
                        scale_last_tile(c, n)
                    if s % 4 == 1 and n < 0 and "back" in parts:
                        scale_last_tile(after(c, -1), NS + n)
                    if s == 8 and "back" in parts: keep_y(after(c, -1))
                    if "end" in parts: end_step(after(c, -2), s, "front" not in parts)
                    if "back" in parts: back_step(after(c, -1), s)
                    if "front" in parts: front_step(after(c, 1), s)
            periods(act, period)

        @block.gpsimd
        def _(pool):
            pool.wait_ge(w_loaded, 16 * 21)
            pool.wait_ge(gn_step, GN_DONE)

            def input_step(c, j):
                wait(pool, sp_step, c, JB * STEPS_SP, STEPS_SP * (j + 1))
                wait(pool, silu_set, c, 2, 1)
                wait(pool, dbu_set, c, NS, 0)
                pool.tensor_tensor(du[:, j, :], delta[:, par(c), j, :], u[:, par(c), j, :],
                                   ALU.mult).then_inc(du_set, 1)

            def times_b(c, n):
                if n == 0:
                    wait(pool, du_set, c, JB, JB)
                wait(pool, bb_in[n % NBB], c, 16 * NS // NBB, 16 * (n // NBB + 1))
                wait(pool, scanned, c, STEPS, 4 * n - 4)
                pool.tensor_tensor(dbu[:, n % 2, :, :], du[:, :, :],
                                   bb[:, n % NBB:n % NBB + 1, :].broadcast_to([P, JB, T]), ALU.mult).then_inc(dbu_set, 1)

            def gate(c, j):
                wait(pool, skip_set, c, JB, j + 1)
                wait(pool, silu_set, c, 2, 2)
                pool.tensor_tensor(u[:, par(c), j, :], u[:, par(c), j, :], sz[:, par(c), j, :],
                                   ALU.mult).then_inc(gated, 1)

            def affine2(c, k):
                wait(pool, nrm_set, c, 3 * Q, 2 * Q)
                wait(pool, affine_step, c, 2, k)
                row = (n2_g, n2_b)[k]
                pool.tensor_tensor(nrm[:, :, :], nrm[:, :, :], row[:, :].unsqueeze(1).broadcast_to([P, Q, DM]),
                                   (ALU.mult, ALU.add)[k]).then_inc(affine_step, 1)

            def residual(c, k):
                wait(pool, xw_in, c, 32, 32)
                wait(pool, rrow_set, c, 1, 1)
                wait(pool, resid_step, c, 3, k)
                v = xw[:, :, :].rearrange("p f (v c) -> p (f v) c", c=CH)
                if k < 2:
                    pool.tensor_tensor(v, v, rrow[:, k * CH:(k + 1) * CH].unsqueeze(1).broadcast_to([P, FB * T // CH, CH]),
                                       (ALU.mult, ALU.add)[k]).then_inc(resid_step, 1)
                else:
                    wait(pool, o_set, c, FB, FB)
                    pool.tensor_tensor(o[:, :, :], o[:, :, :], xw[:, :, :], ALU.add).then_inc(resid_step, 1)

            def end_step(c, n):
                if n in (3, 4): affine2(c, n - 3)
                if n in (7, 8, 9): residual(c, n - 7)

            def back_step(c, n):
                if n in (5, 6):
                    gate(c, 2 * (n - 5))
                    gate(c, 2 * (n - 5) + 1)

            def front_step(c, n):
                if n == 15:
                    for j in range(JB):
                        input_step(c, j)

            front_step((0, 0), NS - 1)

            def period(c, parts):
                for n in range(NS):
                    if "scan" in parts: times_b(c, n)
                    if "end" in parts: end_step(after(c, -2), n)
                    if "back" in parts: back_step(after(c, -1), n)
                    if "front" in parts: front_step(after(c, 1), n)
            periods(pool, period)

        @block.vector
        def _(dve):
            dve.wait_ge(w_loaded, 16 * 21)

            dve.memset(ones, 1.0).then_inc(prep_dve, 1)
            dve.memset(eps[:, 0:2], EPS).then_inc(prep_dve, 1)
            dve.memset(eps[:, 2:3], 1.0).then_inc(prep_dve, 1)
            dve.memset(xd[:, :, :], 1.0).then_inc(prep_dve, 1)
            dve.memset(carry[:, :, :], 0.0).then_inc(prep_dve, 1)
            dve.wait_ge(prep_act, 1)
            dve.tensor_scalar(a_neg[:, :, :], a_neg[:, :, :], -1.0, None, ALU.mult).then_inc(prep_dve, 1)

            def sequence_stats(i):
                for k in range(2):
                    for g in range(8):
                        f, r = g // 4, g % 4
                        wait(dve, seq_turned, (i, k), 8, g + 1)
                        dve.bn_stats(stats[:, f, 2 * i + k, 6 * r:6 * r + 6], ps[:, g, :]).then_inc(seq_stat, 1)
            sequence_stats(0)
            with dve.Fori(1, BATCH // 2) as i:
                sequence_stats(i)
            dve.wait_ge(seq_stat, 8 * BATCH)
            for f in range(FB):
                for b in range(BATCH):
                    dve.bn_aggr(mvs[:, f, b, :], stats[:, f, b, :]).then_inc(gn_aggr, 1)

            dve.wait_ge(gn_aggr, FB * BATCH)
            dve.memset(gn[:, :, :], 0.0).then_inc(gn_step, 1)
            dve.wait_ge(gn_step, 1)
            dve.wait_ge(gn_mm, 1)
            dve.tensor_copy(gn[:, 0, :], ps[:, 0, 0:BATCH]).then_inc(gn_step, 1)
            dve.wait_ge(gn_step, 2)
            for f in range(FB):
                dve.tensor_tensor(gn[:, 1 + f, :], mvs[:, f, :, 0], gn[:, 0, :], ALU.subtract)
            dve.tensor_copy(gn[:, 3, :], gn[:, 0, :]).then_inc(gn_step, 1)
            dve.wait_ge(gn_step, 3)
            dve.tensor_tensor(gn[:, 4, :], gn[:, 1, :], gn[:, 1, :], ALU.mult)
            dve.tensor_tensor(gn[:, 5, :], gn[:, 2, :], gn[:, 2, :], ALU.mult).then_inc(gn_step, 1)
            dve.wait_ge(gn_step, 4)
            dve.tensor_tensor(mvs[:, 0, :, 1], mvs[:, 0, :, 1], gn[:, 4, :], ALU.add).then_inc(gn_step, 1)
            dve.tensor_tensor(mvs[:, 1, :, 1], mvs[:, 1, :, 1], gn[:, 5, :], ALU.add).then_inc(gn_step, 1)
            dve.wait_ge(gn_mm, 2)
            dve.wait_ge(gn_step, 6)
            dve.tensor_scalar(gn[:, 2, :], ps[:, 1, 0:BATCH], EPS, None, ALU.add).then_inc(gn_step, 1)
            dve.wait_ge(gn_root, 2)

            def refine(r, v, t, counter, value):
                value(0)
                dve.tensor_tensor(t, r, r, ALU.mult).then_inc(counter, 1)
                value(1)
                dve.scalar_tensor_tensor(out=t, in0=v[0], scalar=v[1], in1=t, op0=ALU.add, op1=ALU.mult).then_inc(counter, 1)
                value(2)
                dve.tensor_scalar(t, t, -0.5, 1.5, ALU.mult, ALU.add).then_inc(counter, 1)
                value(3)
                dve.tensor_tensor(r, r, t, ALU.mult).then_inc(counter, 1)

            refine(gn[:, 1, :], (gn[:, 2, :], 0.0), gn[:, 3, :], gn_step, lambda k: dve.wait_ge(gn_step, GN_V + k))
            dve.wait_ge(gn_step, GN_V + 4)
            pairs = PAIRS // BATCH
            cv = coef[:, :, :].rearrange("p (b k) e -> p b k e", k=pairs)
            for k in range(pairs):
                dve.tensor_copy(cv[:, :, k, 0], gn[:, 1, :])
                dve.scalar_tensor_tensor(out=cv[:, :, k, 1], in0=gn[:, 0, :], scalar=-1.0, in1=gn[:, 1, :],
                                         op0=ALU.mult, op1=ALU.mult)
                last = dve.tensor_scalar(cv[:, :, k, 2], gn[:, 1, :], 1.0, None, ALU.add)
            last.then_inc(gn_step, 1)
            dve.wait_ge(gn_step, GN_DONE)

            def copy(dst, src):
                return dve.tensor_scalar(dst, src, eps[:, 2:3], None, ALU.mult)

            def set_coef(c):
                wait(dve, xn_set, after(c, -1), FB, 0)
                copy(coef_c[:, par(c), 0:3], coef[:, bass.ds(pair_of(c), 1), 0:3]).then_inc(coef_set, 1)

            def set_mask(c):
                wait(dve, ctx_set, c, 1, 0)
                wait(dve, carried, after(c, -1), NS, 0)
                copy(mask[:, 0:1], starts[:, bass.ds(pair_of(after(c, 1)), 1)]).then_inc(mask_set, 1)

            def set_context(c):
                if is_first(c):
                    dve.memset(xi[:, :, 0:KC - 1], 0.0).then_inc(ctx_set, 1)
                    return
                wait(dve, conv_step, c, JB * (KC - 1), 0)
                wait(dve, tap_set, c, JB, 0)
                wait(dve, xi_set, c, JB, 0)
                m = 1.0
                if par(c) == 0:
                    dve.wait_ge(mask_set, pair_of(after(c, -1)) + 1)
                    m = mask[:, 0:1]
                dve.tensor_scalar(xi[:, :, 0:KC - 1], xi[:, :, T:T + KC - 1], m, None, ALU.mult).then_inc(ctx_set, 1)

            def tap(c, j, k):
                base = (KC - 1) * j + KC - 2 - k
                wait(dve, tap_set, c, JB, j + 1)
                wait(dve, ctx_set, c, 1, 1)
                wait(dve, conv_step, c, JB * (KC - 1), base)
                dve.scalar_tensor_tensor(out=v[:, j, :], in0=xi[:, j, k:k + T], scalar=w_cv[:, j, k:k + 1],
                                         in1=v[:, j, :], op0=ALU.mult, op1=ALU.add).then_inc(conv_step, 1)

            def soft(c, j, k):
                wait(dve, sp_step, c, JB * STEPS_SP, STEPS_SP * j + k)
                if k == 0:
                    wait(dve, sp_exp, c, JB, j + 1)
                    ins = dve.tensor_scalar(sp_m[:, :], sp_e[:, j, :], 1.0, 1.0, ALU.add, ALU.subtract)
                if k == 1:
                    wait(dve, sp_log, c, JB, j + 1)
                    ins = dve.tensor_tensor(sp_m[:, :], sp_l[:, j % 2, :], sp_m[:, :], ALU.subtract)
                if k == 2:
                    ins = dve.scalar_tensor_tensor(out=sp_m[:, :], in0=sp_m[:, :], scalar=0.0, in1=sp_e[:, j, :],
                                                   op0=ALU.min, op1=ALU.add)
                if k == 3:
                    wait(dve, sp_relu, c, JB, j + 1)
                    d = delta[:, par(c), j, :]
                    ins = dve.tensor_tensor(d, d, sp_m[:, :], ALU.add)
                ins.then_inc(sp_step, 1)

            def scan(c, s):
                n, j = s // JB, s % JB
                if j == 0:
                    wait(dve, dbu_set, c, NS, n + 1)
                    wait(dve, turned, c, STEPS, 4 * n - 4)
                    wait(dve, carried, c, NS, n - 1)
                wait(dve, da_set, c, STEPS, s + 1)
                dve.tensor_tensor_scan(h[:, n % 2, j, :], da[:, s % NDA, :], dbu[:, n % 2, j, :],
                                       carry[:, n, j:j + 1], ALU.mult, ALU.add).then_inc(scanned, 1)

            def keep_state(c, n):
                wait(dve, scanned, c, STEPS, 4 * n + 4)
                m = 1.0
                if par(c) == 1:
                    dve.wait_ge(mask_set, pair_of(c) + 1)
                    m = mask[:, 0:1]
                dve.tensor_scalar(carry[:, n, :], h[:, n % 2, :, T - 1], m, None, ALU.mult).then_inc(carried, 1)

            def add_state(c, n, q):
                wait(dve, turned, c, STEPS, 4 * n + q + 1)
                src, dst = turned_bank(n, q), y[:, par(c), q, :]
                cn = cs[:, par(c), q, n:n + 1]
                if n == 0:
                    wait(dve, cs_set, c, 1, 1)
                    wait(dve, back_mm, after(c, -2), GB, K_OUT)
                    dve.tensor_scalar(dst, src, cn, None, ALU.mult).then_inc(summed, 1)
                else:
                    wait(dve, summed, c, NS * QV, QV * (n - 1) + q + 1)
                    dve.scalar_tensor_tensor(out=dst, in0=src, scalar=cn, in1=dst, op0=ALU.mult,
                                             op1=ALU.add).then_inc(summed, 1)

            def diag_r(c, k):
                if k == 0:
                    wait(dve, end_mm, c, GE, 0)
                    wait(dve, rdiag_set, c, 3, 0)
                    copy(coef_e[:, 0:3], coef[:, bass.ds(pair_of(c), 1), 0:3]).then_inc(rdiag_set, 1)
                    wait(dve, rdiag_set, c, 3, 1)
                dve.tensor_scalar(rdiag[:, k * CH:(k + 1) * CH], ident[0:CH, 0:CH],
                                  coef_e[0:CH, 2 - k:3 - k], None, ALU.mult).then_inc(rdiag_set, 1)

            def skip(c, j):
                wait(dve, back_mm, c, GB, K_YT + j + 1)
                if j == 0:
                    wait(dve, front_mm, c, GF, G_C + 1)
                    wait(dve, du_set, c, JB, JB)
                w = u[:, par(c), j, :]
                dve.scalar_tensor_tensor(out=w, in0=w, scalar=d_par[:, j:j + 1],
                                         in1=ps[:, BK0 + (K_YT + j) % 2, :],
                                         op0=ALU.mult, op1=ALU.add).then_inc(skip_set, 1)

            def norm_stats(c, k, g):
                base = LN_NORM * k
                if g == 0:
                    wait(dve, ln_step, c, LN_ALL, base)
                if k < 2:
                    wait(dve, back_mm, c, GB, (K_OUT, K_FF2)[k] + g + 1)
                else:
                    wait(dve, affine_step, c, 2, 2)
                for r in range(2):
                    q = 2 * g + r
                    src = nrm[:, q, :] if k == 2 else ps[:, BK0 + ((K_OUT, K_FF2)[k] + g) % 2, r * DM:(r + 1) * DM]
                    dve.bn_stats(st[:, k, q, :], src).then_inc(ln_step, 1)

            def norm_aggr(c, k):
                for q in range(Q):
                    dve.bn_aggr(mv[:, k, q, :], st[:, k, q, :]).then_inc(ln_step, 1)

            def norm_root(c, k):
                base = LN_NORM * k + 2 * Q
                wait(dve, root_step, c, 6, 2 * k + 2)
                refine(rs[:, k, :], (mv[:, k, :, 1], EPS), rt[:, k, :], ln_step,
                       lambda t: wait(dve, ln_step, c, LN_ALL, base + t))
                wait(dve, ln_step, c, LN_ALL, base + 4)
                dve.scalar_tensor_tensor(out=rt[:, k, :], in0=mv[:, k, :, 0], scalar=-1.0, in1=rs[:, k, :],
                                         op0=ALU.mult, op1=ALU.mult).then_inc(ln_step, 1)

            AGGR_AT = {("end", 4): 1, ("end", 19): 2, ("back", 37): 0}

            def before_scan(kind, c, s):
                k = AGGR_AT[(kind, s)]
                wait(dve, ln_step, c, LN_ALL, LN_NORM * k + Q)
                wait(dve, root_step, c, 6, 2 * k)

            def end_step(c, s):
                if ("end", s) in AGGR_AT: norm_aggr(c, AGGR_AT[("end", s)])
                if s == 0:
                    diag_r(c, 0)
                    diag_r(c, 1)
                if s == 2: norm_stats(c, 1, 1)
                if s == 7: norm_root(c, 1)
                if s in (17, 18): norm_stats(c, 2, s - 17)
                if s == 23: norm_root(c, 2)

            def back_step(c, s):
                if ("back", s) in AGGR_AT: norm_aggr(c, AGGR_AT[("back", s)])
                if s in (13, 14): skip(c, s - 13)
                if s in (18, 19): skip(c, s - 16)
                if s in (31, 36): norm_stats(c, 0, (s - 31) // 5)
                if s == 40: norm_root(c, 0)
                if s == 62: norm_stats(c, 1, 0)

            def front_step(c, s):
                if s == 3: set_coef(c)
                if s == 4: set_context(c)
                if s in (17, 19, 22, 24):
                    tap(c, (17, 19, 22, 24).index(s), 2)
                    tap(c, (17, 19, 22, 24).index(s), 1)
                if s in (18, 20, 23, 25): tap(c, (18, 20, 23, 25).index(s), 0)
                if s in (47, 49, 51, 53): soft(c, (47, 49, 51, 53).index(s), 0)
                if s in (48, 50, 52, 54):
                    j = (48, 50, 52, 54).index(s)
                    soft(c, j, 1)
                    soft(c, j, 2)
                    soft(c, j, 3)

            for s in range(STEPS):
                front_step((0, 0), s)

            def period(c, parts):
                if par(c) == 1 and "scan" in parts:
                    set_mask(c)
                for s in range(STEPS):
                    for kind, d in (("end", -2), ("back", -1)):
                        if kind in parts and (kind, s) in AGGR_AT:
                            before_scan(kind, after(c, d), s)
                            if "scan" not in parts:
                                dve.tensor_copy(eps[:, 1:2], eps[:, 0:1])
                    if "scan" in parts: scan(c, s)
                    if s % 4 == 0 and s > 0 and "scan" in parts:
                        keep_state(c, s // 4 - 1)
                    if s == 0 and "back" in parts and "scan" in parts:
                        keep_state(after(c, -1), NS - 1)
                    n, q = (s - LAG) // Q, (s - LAG) % Q
                    if q < QV and n >= 0 and "scan" in parts:
                        add_state(c, n, q)
                    if q < QV and n < 0 and "back" in parts:
                        add_state(after(c, -1), NS + n, q)
                    if "end" in parts: end_step(after(c, -2), s)
                    if "back" in parts: back_step(after(c, -1), s)
                    if "front" in parts: front_step(after(c, 1), s)
            periods(dve, period)


def kernel(**inputs):
    import numpy as np
    import concourse.bacc as bacc
    from concourse import mybir as mb
    from concourse.bass_utils import run_bass_kernel_spmd as run

    def w(name):
        return np.asarray(inputs["L0_conv_" + name])

    def cols(v):
        return v.reshape(-1, P).T

    f = np.arange(P)
    avg = ((f[:, None] % CH) // 2 == (f[None, :] % CH) // 2) / np.float32(8)
    per_seq = PAIRS // BATCH
    inner = (np.arange(PAIRS + 1) % per_seq != 0)[None, :] * np.ones((P, 1))
    consts = np.concatenate([np.eye(P), avg, inner], axis=1).astype(np.float32)

    x_proj = w("x_proj_w").T
    wx = np.zeros((DI, 96 + R), x_proj.dtype)
    wx[:, 0:NS] = x_proj[:, R:R + NS]
    wx[:, 96:96 + R] = x_proj[:, 0:R]
    arrays = {
        "x": np.asarray(inputs["x"]), "consts": consts, "win_t": w("in_proj_w").T, "bin_c": cols(w("in_proj_b")),
        "convw": w("conv_w"), "convb": cols(w("conv_b")), "wx": wx, "wc": x_proj[:, R + NS:],
        "wdt": np.concatenate([w("dt_proj_w").T, w("dt_proj_b")[None, :]], axis=0), "alog": w("A_log"),
        "dpar": cols(w("Dp")), "wout": w("out_proj_w").T, "n1g": cols(w("norm1_g")), "n1b": cols(w("norm1_b")),
        "wf1": w("ffn1_w").T, "bf1": cols(w("ffn1_b")), "wf2": w("ffn2_w").T, "bf2": w("ffn2_b"),
        "g2rows": np.tile(w("norm2_g"), (P, 1)), "b2rows": np.tile(w("norm2_b"), (P, 1)),
        "lng": cols(w("ln_g")), "lnb": cols(w("ln_b")),
    }
    nc = bacc.Bacc("TRN2", target_bir_lowering=False, num_devices=1)
    data, args = {}, []
    for name, a in arrays.items():
        a = np.ascontiguousarray(a)
        data[f"in_{name}"] = a
        args.append(nc.dram_tensor(f"in_{name}", a.shape, mb.dt.from_np(a.dtype), kind="ExternalInput").ap())
    args.append(nc.dram_tensor("out_0", (16, 32, 256, 64), mb.dt.float32, kind="ExternalOutput").ap())
    layer_kernel(nc, *args)
    r = run(nc, [data], core_ids=[0])
    return r.results[0]["out_0"]
```
